# Optimizing a Trainium2 kernel written in Bass

```python
import numpy as np
import jax
import jax.numpy as jnp

def _softmax(x, axis=-1):
    return jax.nn.softmax(x, axis=axis)

def _gelu(x):
    return jax.nn.gelu(x, approximate=True)

def _silu(x):
    return jax.nn.silu(x)

def _sigmoid(x):
    return jax.nn.sigmoid(x)

def _layernorm(x, axis=-1, eps=1e-05):
    m = jnp.mean(x, axis=axis, keepdims=True)
    v = jnp.var(x, axis=axis, keepdims=True)
    return (x - m) / jnp.sqrt(v + eps)

def _scatter_add(tgt, idx, src, axis=0):
    return tgt.at[idx].add(src)

def _segment_sum(src, seg, n):
    return jax.ops.segment_sum(src, seg, n)
kernel_name = 'mk_conv_preact_d2_conv_nhwc768_r4_ce2305'

def setup_inputs(seed: int=0):
    np.random.seed(seed)
    _w = jnp.asarray

    def _rec_inputs():
        import jax
        import jax.numpy as jnp
        _gk = jax.random.key(seed)
        x = -0.0001476 + 0.9999 * jax.random.normal(jax.random.fold_in(_gk, 1), (64, 14, 14, 192), jnp.float32)
        return x
    x = _rec_inputs()

    def _L0_conv_setup():
        import jax, jax.numpy as jnp
        import numpy as np
        NUM_HEADS = 12
        HEAD_DIM = 16

        def _rel_pos_table(size, rel_pos):
            coords = jnp.arange(size)[:, None] - jnp.arange(size)[None, :] + (size - 1)
            return rel_pos[coords]
        key = jax.random.key(seed)
        ks = jax.random.split(key, 7)
        B, H, W, C = (64, 14, 14, 192)
        return {'hidden_states': jax.random.normal(ks[0], (B, H, W, C), jnp.float32), 'qkv_w': jax.random.normal(ks[1], (3 * C, C), jnp.float32) * 0.02, 'qkv_b': jax.random.normal(ks[2], (3 * C,), jnp.float32) * 0.02, 'rel_pos_h': jax.random.normal(ks[3], (2 * H - 1, HEAD_DIM), jnp.float32) * 0.02, 'rel_pos_w': jax.random.normal(ks[4], (2 * W - 1, HEAD_DIM), jnp.float32) * 0.02, 'proj_w': jax.random.normal(ks[5], (C, C), jnp.float32) * 0.02, 'proj_b': jax.random.normal(ks[6], (C,), jnp.float32) * 0.02}
    _L0_conv_all = _L0_conv_setup()
    _L0_conv_in = {k: v for k, v in _L0_conv_all.items() if k in ('qkv_w', 'qkv_b', 'rel_pos_h', 'rel_pos_w', 'proj_w', 'proj_b')}
    del _L0_conv_all

    def _L1_conv_setup():
        import jax, jax.numpy as jnp
        import numpy as np
        B, H, W, DIM = (8, 32, 32, 192)
        NUM_HEADS = 12
        HEAD_DIM = DIM // NUM_HEADS
        key = jax.random.key(seed)
        ks = jax.random.split(key, 7)
        x = jax.random.normal(ks[0], (B, H, W, DIM), dtype=jnp.float32)
        qkv_w = jax.random.normal(ks[1], (DIM, 3 * DIM), dtype=jnp.float32) * 0.02
        qkv_b = jnp.zeros((3 * DIM,), dtype=jnp.float32)
        proj_w = jax.random.normal(ks[2], (DIM, DIM), dtype=jnp.float32) * 0.02
        proj_b = jnp.zeros((DIM,), dtype=jnp.float32)
        rel_pos_h = jax.random.normal(ks[3], (2 * H - 1, HEAD_DIM), dtype=jnp.float32) * 0.02
        rel_pos_w = jax.random.normal(ks[4], (2 * W - 1, HEAD_DIM), dtype=jnp.float32) * 0.02
        return {'x': x, 'qkv_w': qkv_w, 'qkv_b': qkv_b, 'proj_w': proj_w, 'proj_b': proj_b, 'rel_pos_h': rel_pos_h, 'rel_pos_w': rel_pos_w}
    _L1_conv_all = _L1_conv_setup()
    _L1_conv_in = {k: v for k, v in _L1_conv_all.items() if k in ('qkv_w', 'qkv_b', 'proj_w', 'proj_b', 'rel_pos_h', 'rel_pos_w')}
    del _L1_conv_all
    return {'x': x, 'L0_conv_qkv_w': _L0_conv_in['qkv_w'], 'L0_conv_qkv_b': _L0_conv_in['qkv_b'], 'L0_conv_rel_pos_h': _L0_conv_in['rel_pos_h'], 'L0_conv_rel_pos_w': _L0_conv_in['rel_pos_w'], 'L0_conv_proj_w': _L0_conv_in['proj_w'], 'L0_conv_proj_b': _L0_conv_in['proj_b'], 'L1_conv_qkv_w': _L1_conv_in['qkv_w'], 'L1_conv_qkv_b': _L1_conv_in['qkv_b'], 'L1_conv_proj_w': _L1_conv_in['proj_w'], 'L1_conv_proj_b': _L1_conv_in['proj_b'], 'L1_conv_rel_pos_h': _L1_conv_in['rel_pos_h'], 'L1_conv_rel_pos_w': _L1_conv_in['rel_pos_w']}

def reference(x, L0_conv_qkv_w, L0_conv_qkv_b, L0_conv_rel_pos_h, L0_conv_rel_pos_w, L0_conv_proj_w, L0_conv_proj_b, L1_conv_qkv_w, L1_conv_qkv_b, L1_conv_proj_w, L1_conv_proj_b, L1_conv_rel_pos_h, L1_conv_rel_pos_w):
    import jax
    import jax.numpy as jnp

    def _L0_conv_ref(hidden_states, qkv_w, qkv_b, rel_pos_h, rel_pos_w, proj_w, proj_b):
        import jax, jax.numpy as jnp
        import numpy as np
        NUM_HEADS = 12
        HEAD_DIM = 16

        def _rel_pos_table(size, rel_pos):
            coords = jnp.arange(size)[:, None] - jnp.arange(size)[None, :] + (size - 1)
            return rel_pos[coords]
        B, H, W, C = hidden_states.shape
        nh, hd = (NUM_HEADS, C // NUM_HEADS)
        scale = hd ** (-0.5)
        HW = H * W
        qkv = hidden_states.reshape(B, HW, C) @ qkv_w.T + qkv_b
        qkv = qkv.reshape(B, HW, 3, nh, hd).transpose(2, 0, 3, 1, 4)
        qkv = qkv.reshape(3, B * nh, HW, hd)
        q, k, v = (qkv[0], qkv[1], qkv[2])
        attn = jnp.einsum('bqd,bkd->bqk', q * scale, k)
        Rh = _rel_pos_table(H, rel_pos_h)
        Rw = _rel_pos_table(W, rel_pos_w)
        qr = q.reshape(B * nh, H, W, hd)
        rel_h = jnp.einsum('bhwc,hkc->bhwk', qr, Rh)
        rel_w = jnp.einsum('bhwc,wkc->bhwk', qr, Rw)
        attn = attn.reshape(B * nh, H, W, H, W) + rel_h[:, :, :, :, None] + rel_w[:, :, :, None, :]
        attn = attn.reshape(B * nh, HW, HW)
        attn = jax.nn.softmax(attn.astype(jnp.float32), axis=-1).astype(q.dtype)
        out = jnp.einsum('bqk,bkd->bqd', attn, v)
        out = out.reshape(B, nh, H, W, hd).transpose(0, 2, 3, 1, 4).reshape(B, H, W, C)
        out = out @ proj_w.T + proj_b
        return out

    def _L1_conv_ref(x, qkv_w, qkv_b, proj_w, proj_b, rel_pos_h, rel_pos_w):
        import jax, jax.numpy as jnp
        import numpy as np
        B, H, W, DIM = (8, 32, 32, 192)
        NUM_HEADS = 12
        HEAD_DIM = DIM // NUM_HEADS
        b, h, w, dim = x.shape
        nH, hd = (NUM_HEADS, dim // NUM_HEADS)
        scale = hd ** (-0.5)
        hw = h * w
        qkv = x.reshape(b, hw, dim) @ qkv_w + qkv_b
        qkv = qkv.reshape(b, hw, 3, nH, hd).transpose(2, 0, 3, 1, 4)
        qkv = qkv.reshape(3, b * nH, hw, hd)
        q, k, v = (qkv[0], qkv[1], qkv[2])
        idx_h = jnp.arange(h)[:, None] - jnp.arange(h)[None, :] + (h - 1)
        idx_w = jnp.arange(w)[:, None] - jnp.arange(w)[None, :] + (w - 1)
        Rh = rel_pos_h[idx_h]
        Rw = rel_pos_w[idx_w]
        r_q = q.reshape(b * nH, h, w, hd)
        rel_h = jnp.einsum('bhwc,hkc->bhwk', r_q, Rh)
        rel_w = jnp.einsum('bhwc,wkc->bhwk', r_q, Rw)
        attn_bias = (rel_h[:, :, :, :, None] + rel_w[:, :, :, None, :]).reshape(b * nH, hw, hw)
        attn = jnp.einsum('bqd,bkd->bqk', q, k) * scale + attn_bias
        attn = jax.nn.softmax(attn, axis=-1)
        out = jnp.einsum('bqk,bkd->bqd', attn, v)
        out = out.reshape(b, nH, h, w, hd).transpose(0, 2, 3, 1, 4).reshape(b, h, w, dim)
        return out @ proj_w + proj_b

    def _gn(v, G=32, eps=1e-05):
        B_, H_, W_, C_ = v.shape
        g = v.reshape(B_, H_, W_, G, C_ // G)
        m = jnp.mean(g, axis=(1, 2, 4), keepdims=True)
        s = jnp.var(g, axis=(1, 2, 4), keepdims=True)
        return ((g - m) / jnp.sqrt(s + eps)).reshape(v.shape)

    def _ln_c(v, eps=1e-06):
        m = jnp.mean(v, axis=-1, keepdims=True)
        s = jnp.var(v, axis=-1, keepdims=True)
        return (v - m) / jnp.sqrt(s + eps)

    def _ln_t(v, eps=1e-05):
        m = jnp.mean(v, axis=-1, keepdims=True)
        s = jnp.var(v, axis=-1, keepdims=True)
        return (v - m) / jnp.sqrt(s + eps)

    def _to_tokens(v):
        B_, H_, W_, C_ = v.shape
        return v.reshape(B_, H_ * W_, C_)

    def _from_tokens(t, like):
        return t.reshape(like.shape)
    x = x + _L0_conv_ref(_gn(x), L0_conv_qkv_w, L0_conv_qkv_b, L0_conv_rel_pos_h, L0_conv_rel_pos_w, L0_conv_proj_w, L0_conv_proj_b)
    x = x + _L1_conv_ref(_gn(x), L1_conv_qkv_w, L1_conv_qkv_b, L1_conv_proj_w, L1_conv_proj_b, L1_conv_rel_pos_h, L1_conv_rel_pos_w)
    return x

_drawn_inputs = setup_inputs


def setup_inputs(seed=0):
    import zlib

    import numpy as np

    out = dict(_drawn_inputs(seed))
    spreads = {'L1_conv_qkv_b': (0.0, 0.497), 'L1_conv_proj_b': (0.0, 0.285)}
    factors = {'L0_conv_qkv_w': 8.0,
     'L0_conv_qkv_b': 8.0,
     'L0_conv_rel_pos_h': 8.0,
     'L0_conv_rel_pos_w': 8.0,
     'L0_conv_proj_w': 7.258,
     'L0_conv_proj_b': 9.053,
     'L1_conv_qkv_w': 8.0,
     'L1_conv_rel_pos_h': 8.0,
     'L1_conv_rel_pos_w': 8.0}
    for name, (base, spread) in spreads.items():
        noise = np.random.default_rng([zlib.crc32(name.encode()), seed]).standard_normal(out[name].shape)
        drawn = base * np.exp(spread * noise) if base else spread * noise
        out[name] = jnp.asarray(drawn.astype(out[name].dtype))
    for name, factor in factors.items():
        out[name] = (out[name] * factor).astype(out[name].dtype)
    return out
```

```python
from contextlib import ExitStack

import concourse.bass as bass
from concourse import mybir

F32 = mybir.dt.float32
F16 = mybir.dt.float16
ALU = mybir.AluOpType
ACT = mybir.ActivationFunctionType
AX = mybir.AxisListType

LAYERS = 2
SAMPLES = 64
UNITS = LAYERS * SAMPLES
SIDE = 14
TOK = SIDE * SIDE
HT = TOK // 2
HALF = SIDE // 2
C = 192
CC = C // 2
HEADS = 12
HC = HEADS // 2
HD = C // HEADS
GROUP = C // 32
EPS = 1e-5
REL = 2 * SIDE - 1

QS = 32.0
KS = 32.0
RS = 4.0
VS = 32.0

R_REL = 4 * HD
R_MAX = R_REL + 4 * SIDE
STACK = R_MAX + 1

PW = 32
HG = 4
GROUPS = HEADS // HG
PRING = 8
RELB = (3, 3, 1)
RP = SIDE - 1 + 32
UNROLL = 4


class Unit:

    def __init__(self, block, place):
        self.block = block + place // UNROLL
        self.r = place % UNROLL
        self.n = self.block * UNROLL + self.r
        self.fixed = isinstance(block, int)


def attention_kernel(nc, x, w_all, b_qk, b_rows, rel, onehot, ident_in, gmat_in, out):
    with ExitStack() as ctx:
        def sb(name, shape, dt=F32):
            return ctx.enter_context(nc.sbuf_tensor(name, shape, dt))

        def psum(name, shape):
            return ctx.enter_context(nc.psum_tensor(name, shape, F32))

        def sem(name):
            return ctx.enter_context(nc.semaphore(name))

        def sems(name, n=UNROLL):
            return [sem(f"{name}{i}") for i in range(n)]

        x1 = nc.dram_tensor("x1", [SAMPLES, TOK, C], F32).ap()
        q_dram = nc.dram_tensor("q_dram", [UNROLL, 2, 2, 2, CC, HT], F16).ap()
        k_dram = nc.dram_tensor("k_dram", [UNROLL, 2, 2, CC, TOK], F16).ap()

        ident = sb("ident", [128, 128])
        gmat = sb("gmat", [CC, CC])
        w_raw = sb("w_raw", [CC, 2, 4 * C])
        w_hi = sb("w_hi", [CC, LAYERS, 2, 4 * C], F16)
        w_lo = sb("w_lo", [CC, LAYERS, 2, 4 * C], F16)
        bqk_raw = sb("bqk_raw", [CC, LAYERS, 4])
        bqk = sb("bqk", [CC, LAYERS, 4])
        brow = sb("brow", [HT, LAYERS, 2, C])
        rel_raw = sb("rel_raw", [64, LAYERS, 2, RP])
        rel_st = sb("rel_st", [64, LAYERS, 2, RP], F16)
        oh_raw = sb("oh_raw", [128, TOK])
        halfpow = sb("halfpow", [CC, 2])
        eps = sb("eps", [CC, 2])
        anchor = sb("anchor", [CC, 3])

        q_st = [sb(f"q_st{i}", [128, 2, HEADS, HT], F16) for i in range(4)]
        k_st = [sb(f"k_st{i}", [128, HEADS, TOK], F16) for i in range(4)]
        v_st = [sb(f"v_st{i}", [HT, 2, HEADS, PW]) for i in range(4)]

        def pair(name, shape, dt=F32):
            return [sb(f"{name}{i}", shape, dt) for i in range(2)]

        xa = pair("xa", [HT, 2, C])
        xT = pair("xT", [CC, 2, TOK])
        bn6 = pair("bn6", [CC, 2, 6])
        mv = pair("mv", [CC, 2, 2])
        gsm = pair("gsm", [CC, 2, 2])
        msq = pair("msq", [CC, 2])
        gvar = pair("gvar", [CC, 2])
        rstd = pair("rstd", [CC, 2])
        nmean = pair("nmean", [CC, 2])
        xn = pair("xn", [CC, 2, TOK])
        xn_hi = pair("xn_hi", [CC, 2, TOK], F16)
        xn_lo = pair("xn_lo", [CC, 2, TOK], F16)
        q_hi = pair("q_hi", [CC, 2, TOK], F16)
        q_lo = pair("q_lo", [CC, 2, TOK], F16)
        k_hi = pair("k_hi", [CC, 2, TOK], F16)
        k_lo = pair("k_lo", [CC, 2, TOK], F16)
        rel_hi = pair("rel_hi", [128, HEADS, HT], F16)
        rel_lo = pair("rel_lo", [128, HEADS, HT], F16)
        mx = pair("mx", [HT, 2, HEADS])
        mrow = pair("mrow", [2 * HEADS, HT], F16)
        probs = [sb(f"probs{i}", [HT, 2, TOK]) for i in range(PRING)]
        o_sb = pair("o_sb", [128, GROUPS, TOK])
        rsum = pair("rsum", [HT, 2, HEADS])
        on = pair("on", [HT, 2, C])
        oT_hi = pair("oT_hi", [CC, 2, TOK], F16)
        oT_lo = pair("oT_lo", [CC, 2, TOK], F16)
        xd = pair("xd", [HT, 2, C])
        xb = pair("xb", [HT, 2, C])
        yo = pair("yo", [HT, 2, C])

        ps_max = [psum(f"ps_max{i}", [128, 512]) for i in range(2)]
        ps_sc = [psum(f"ps_sc{i}", [128, 512]) for i in range(2)]
        ps_o = [psum(f"ps_o{i}", [128, 512]) for i in range(2)]
        ps_m = [psum(f"ps_m{i}", [128, 512]) for i in range(2)]

        s_const = sem("s_const")
        s_wraw = sems("s_wraw", 2)
        s_pad = sem("s_pad")
        s_wsc = sem("s_wsc")
        s_whi = sem("s_whi")
        s_wlo = sem("s_wlo")
        s_setup = sem("s_setup")
        s_x = sems("s_x")
        s_xT_ps = sem("s_xT_ps")
        s_xT = sem("s_xT")
        s_bn = sem("s_bn")
        s_agg = sem("s_agg")
        s_sq = sem("s_sq")
        s_mv = sem("s_mv")
        s_g_ps = sem("s_g_ps")
        s_g = sem("s_g")
        s_gp = sem("s_gp")
        s_xn = sem("s_xn")
        s_xhi = sem("s_xhi")
        s_xlo = sem("s_xlo")
        s_q_ps = sem("s_q_ps")
        s_k_ps = sem("s_k_ps")
        s_v_ps = sem("s_v_ps")
        s_qhi = sem("s_qhi")
        s_khi = sem("s_khi")
        s_qlo = sem("s_qlo")
        s_klo = sem("s_klo")
        s_v = sem("s_v")
        s_qkd = sems("s_qkd")
        s_qk = sems("s_qk")
        s_rel_ps = sem("s_rel_ps")
        s_rhi = sem("s_rhi")
        s_rlo = sem("s_rlo")
        s_rel = sems("s_rel")
        s_sm_ps = sem("s_sm_ps")
        s_mx = sem("s_mx")
        s_mT_ps = sem("s_mT_ps")
        s_mrow = sem("s_mrow")
        s_m = sems("s_m")
        s_sc_ps = sem("s_sc_ps")
        s_p = sem("s_p")
        s_o_ps = sem("s_o_ps")
        s_o = sem("s_o")
        s_ot_ps = sem("s_ot_ps")
        s_rs = sem("s_rs")
        s_on = sem("s_on")
        s_oT_ps = sem("s_oT_ps")
        s_ohi = sem("s_ohi")
        s_olo = sem("s_olo")
        s_y_ps = sem("s_y_ps")
        s_xd = sems("s_xd")
        s_xb = sem("s_xb")
        s_y = sem("s_y")
        s_out = sems("s_out")

        QK_PARTS = 16 * 16
        block = ctx.enter_context(nc.Block())

        def wait(eng, s, value):
            if not (isinstance(value, int) and value <= 0):
                eng.wait_ge(s, value)

        def wait_dma(eng, group, u, dmas=1):
            wait(eng, group[u.r], (u.block + 1) * (16 * dmas))

        def active(u):
            return not u.fixed or 0 <= u.n < UNITS

        def layer_of(u, loop_layer):
            return loop_layer if not u.fixed else u.n // SAMPLES

        def run(eng, iteration):
            for layer in range(LAYERS):
                edge = UNROLL * (2 if layer == 0 else 1)
                first = layer * SAMPLES
                for i in range(first, first + edge):
                    iteration(lambda lag, i=i: Unit(0, i - lag), layer)
                with eng.Fori((first + edge) // UNROLL, (first + SAMPLES) // UNROLL) as t:
                    for r in range(UNROLL):
                        iteration(lambda lag, t=t, r=r: Unit(t, r - lag), layer)
            for i in range(UNITS, UNITS + UNROLL):
                iteration(lambda lag, i=i: Unit(0, i - lag), LAYERS - 1)

        LAG_A, LAG_REL, LAG_MAX, LAG_MT, LAG_C, LAG_D = 0, 1, 2, 3, 3, 4
        SHIFT = 4

        def c_step(unit, s):
            return (unit(LAG_C), s - SHIFT) if s >= SHIFT else (unit(LAG_C + 1), s - SHIFT + HEADS)

        PV_SLOT = {}
        for g in range(GROUPS):
            for kt in range(2):
                at = SHIFT + HG * g + HG + 1 + kt
                PV_SLOT[at % HEADS] = (LAG_C + at // HEADS, g, kt)

        JOBS = {1: ["mT"], 3: ["xT", "rel0"], 4: ["g"], 5: ["rel1"], 6: ["rel2"], 8: ["ot0", "ot1"],
                9: ["q"], 10: ["oT", "k"], 11: ["v", "y"]}
        BANK = {"mT": 0, "xT": 1, "rel0": 0, "g": 1, "rel1": 0, "rel2": 1, "ot0": 0, "ot1": 1,
                "q": 0, "oT": 1, "k": 0, "v": 1, "y": 0}
        LAG = {"mT": LAG_MT, "xT": LAG_A, "g": LAG_A, "q": LAG_A, "k": LAG_A, "v": LAG_A,
               "rel0": LAG_REL, "rel1": LAG_REL, "rel2": LAG_REL,
               "ot0": LAG_D, "ot1": LAG_D, "oT": LAG_D, "y": LAG_D}
        READ = {"mT": (s_mrow, 1, 1), "xT": (s_xT, 1, 1), "g": (s_g, 1, 1),
                "rel0": (s_rlo, 6, 2), "rel1": (s_rlo, 6, 4), "rel2": (s_rlo, 6, 6),
                "ot0": (s_on, 2, 1), "ot1": (s_on, 2, 2), "q": (s_qlo, 2, 2), "k": (s_klo, 2, 2),
                "v": (s_v, 1, 1), "oT": (s_olo, 1, 1), "y": (s_y, 1, 1)}
        ORDER = [j for s in sorted(JOBS) for j in JOBS[s]]

        def bank_free(pe, unit, job):
            at = ORDER.index(job)
            for back in range(1, 3 * len(ORDER)):
                turns, k = divmod(at - back, len(ORDER))
                before = ORDER[k]
                if BANK[before] != BANK[job]:
                    continue
                u = unit(LAG[before] - turns)
                if active(u):
                    s, per, which = READ[before]
                    wait(pe, s, u.n * per + which)
                    return

        def rel_views(dst, ps, rows, a0):
            by_row = (dst[0:64, :, a0 * SIDE:(a0 + rows) * SIDE].rearrange("p h (a b) -> p a h b", a=rows),
                      ps[0:64, 0:rows * HEADS * SIDE].rearrange("p (a h b) -> p a h b", a=rows, h=HEADS))
            w = 2 * rows
            by_col = (dst[64:128, :, :].rearrange("p h (a b) -> p b h a", a=HALF)[:, 2 * a0:2 * a0 + w],
                      ps[64:128, 0:w * HEADS * HALF].rearrange("p (b h a) -> p b h a", b=w, h=HEADS))
            return by_row, by_col

        @block.sync
        def _(sp):
            sp.dma_start(ident[:, :], ident_in).then_inc(s_const, 16)
            sp.dma_start(gmat[:, :], gmat_in).then_inc(s_const, 16)
            sp.dma_start(oh_raw[R_REL:STACK, :], onehot).then_inc(s_const, 16)
            sp.dma_start(bqk_raw[:, :, :], b_qk).then_inc(s_const, 16)
            sp.dma_start(brow[:, :, :, :], b_rows).then_inc(s_const, 16)
            sp.wait_ge(s_pad, 1)
            sp.dma_start(rel_raw[:, :, :, 0:REL], rel).then_inc(s_const, 16)
            for layer in range(LAYERS):
                if layer:
                    sp.wait_ge(s_wlo, layer)
                sp.dma_start(w_raw[:, :, :], w_all[layer].rearrange("(c p) n -> p c n", c=2))\
                  .then_inc(s_wraw[layer], 16)

            def tokens(dram):
                return dram.rearrange("o (h t) c -> t (o h) c", h=2)

            def iteration(unit, layer):
                u = unit(LAG_A)
                if active(u):
                    src_layer = layer
                    if src_layer:
                        before = unit(SAMPLES)
                        wait_dma(sp, s_out, before)
                    src, at = (x, u.n) if not src_layer else (x1, u.n - SAMPLES)
                    wait(sp, s_xT_ps, u.n - 1)
                    sp.dma_start(xa[u.r % 2][:, :, :], tokens(src[bass.ds(at, 1)])).then_inc(s_x[u.r], 16)
                d = unit(LAG_D)
                if active(d):
                    dl = layer_of(d, layer)
                    src, at = (x, d.n) if not dl else (x1, d.n - SAMPLES)
                    wait(sp, s_xb, d.n - 1)
                    sp.dma_start(xd[d.r % 2][:, :, :], tokens(src[bass.ds(at, 1)])).then_inc(s_xd[d.r], 16)
                m = unit(LAG_MT)
                if active(m):
                    wait(sp, s_mrow, m.n + 1)
                    sp.dma_start(q_st[m.r][R_MAX:STACK, :, :, :], mrow[m.r % 2][:, :]).then_inc(s_m[m.r], 16)
                e = unit(LAG_REL)
                if active(e):
                    wait(sp, s_rlo, e.n * 6 + 6)
                    for part, row in ((rel_hi, R_REL), (rel_lo, R_REL + 2 * SIDE)):
                        for axis in range(2):
                            for half in range(2):
                                p = 64 * axis + 32 * half
                                r0 = row + axis * SIDE
                                sp.dma_start(q_st[e.r][r0:r0 + SIDE, half, :, :],
                                             part[e.r % 2][p:p + SIDE, :, :]).then_inc(s_rel[e.r], 16)
                if active(u):
                    wait(sp, s_sc_ps, (u.n - 3) * HEADS)
                    wait(sp, s_qlo, u.n * 2 + 2)
                    for hl, part in enumerate((q_hi, q_lo)):
                        for c in range(2):
                            sp.dma_start(q_dram[u.r, hl, :, c].rearrange("q p t -> p q t"),
                                         part[u.r % 2][:, c, :].rearrange("p (q t) -> p q t", q=2))\
                              .then_inc(s_qkd[u.r], 16)
                    wait(sp, s_klo, u.n * 2 + 2)
                    for hl, part in enumerate((k_hi, k_lo)):
                        sp.dma_start(k_dram[u.r, hl].rearrange("c p t -> p c t"),
                                     part[u.r % 2][:, :, :]).then_inc(s_qkd[u.r], 16)
                    wait_dma(sp, s_qkd, u, 6)
                    for g in range(4):
                        rows = slice(HD * g, HD * g + HD)
                        sp.dma_start(q_st[u.r][rows, :, :, :].rearrange("d q (c h) t -> d (q c) (h t)", c=2),
                                     q_dram[u.r, g % 2].rearrange("q c (d h) t -> d (q c) (h t)", d=HD))\
                          .then_inc(s_qk[u.r], 16)
                        sp.dma_start(k_st[u.r][rows, :, :].rearrange("d (c h) t -> d c (h t)", c=2),
                                     k_dram[u.r, g // 2].rearrange("c (d h) t -> d c (h t)", d=HD))\
                          .then_inc(s_qk[u.r], 16)
                if active(d):
                    wait(sp, s_y, d.n + 1)
                    dl = layer_of(d, layer)
                    dst, at = (x1, d.n) if not dl else (out, d.n - SAMPLES)
                    sp.dma_start(tokens(dst[bass.ds(at, 1)]), yo[d.r % 2][:, :, :]).then_inc(s_out[d.r], 16)

            run(sp, iteration)
            for r in range(UNROLL):
                sp.wait_ge(s_out[r], 16 * UNITS // UNROLL)

        @block.tensor
        def _(pe):
            pe.wait_ge(s_setup, 1)
            pe.wait_ge(s_const, 16 * 6)

            def split_product(dst, weights, moving, signal):
                terms = [(a, b, c) for c in range(2) for a, b in ((0, 0), (0, 1), (1, 0))]
                for n, (a, b, c) in enumerate(terms):
                    last = nc.tensor.matmul(dst, weights(a, c), moving(b, c),
                                            start=n == 0, stop=n == len(terms) - 1)
                if signal is not None:
                    last.then_inc(signal, 1)

            def job(name, unit, layer):
                u = unit(LAG[name])
                if not active(u):
                    return
                lay = layer_of(u, layer)
                ps, p2 = ps_m[BANK[name]], u.r % 2
                w_part, x_part = (w_hi, w_lo), (xn_hi[p2], xn_lo[p2])
                if name == "xT":
                    wait_dma(pe, s_x, u)
                    bank_free(pe, unit, name)
                    for c in range(2):
                        for h in range(2):
                            last = nc.tensor.transpose(ps[0:CC, c * TOK + h * HT:c * TOK + h * HT + HT],
                                                       xa[p2][:, h, c * CC:c * CC + CC], ident[0:HT, 0:HT])
                    last.then_inc(s_xT_ps, 1)
                elif name == "g":
                    pe.wait_ge(s_mv, u.n + 1)
                    bank_free(pe, unit, name)
                    nc.tensor.matmul(ps[0:CC, 0:4], gmat[:, :], mv[p2][:, :, :], start=True, stop=True)\
                      .then_inc(s_g_ps, 1)
                elif name in ("q", "k"):
                    pe.wait_ge(s_xlo, u.n + 1)
                    bank_free(pe, unit, name)
                    for m in range(2):
                        n0 = (2 * (name == "k") + m) * CC
                        split_product(ps[0:CC, m * TOK:m * TOK + TOK],
                                      lambda a, c: w_part[a][:, lay, c, n0:n0 + CC],
                                      lambda b, c: x_part[b][:, c, :],
                                      (s_q_ps if name == "q" else s_k_ps) if m else None)
                elif name == "v":
                    pe.wait_ge(s_xlo, u.n + 1)
                    bank_free(pe, unit, name)
                    for h in range(2):
                        split_product(ps[0:HT, h * C:h * C + C],
                                      lambda a, c: x_part[a][:, c, h * HT:h * HT + HT],
                                      lambda b, c: w_part[b][:, lay, c, 2 * C:3 * C],
                                      s_v_ps if h else None)
                elif name.startswith("rel"):
                    n = int(name[3])
                    rows = RELB[n]
                    if n == 0:
                        wait_dma(pe, s_qk, u, 8)
                    bank_free(pe, unit, name)
                    nc.tensor.matmul(ps[0:CC, 511:512], w_hi[:, 0, 0, 0:CC], w_hi[:, 0, 0, 0:1],
                                     start=True, stop=True)
                    a0 = sum(RELB[:n])
                    for a in range(rows):
                        for half in range(2):
                            ah = half * HALF + a0 + a
                            last = nc.tensor.matmul(
                                ps[32 * half:32 * half + 32, a * HEADS * SIDE:(a + 1) * HEADS * SIDE],
                                rel_st[:, lay, 0, SIDE - 1 - ah:SIDE - 1 - ah + 32],
                                q_st[u.r][0:R_REL, half, :, (a0 + a) * SIDE:(a0 + a + 1) * SIDE],
                                start=True, stop=True)
                    w = 2 * rows
                    for b in range(2 * a0, 2 * a0 + w):
                        for half in range(2):
                            at = (b - 2 * a0) * HEADS * HALF
                            last = nc.tensor.matmul(
                                ps[64 + 32 * half:96 + 32 * half, at:at + HEADS * HALF],
                                rel_st[:, lay, 1, SIDE - 1 - b:SIDE - 1 - b + 32],
                                q_st[u.r][0:R_REL, half, :, b::SIDE],
                                start=True, stop=True)
                    last.then_inc(s_rel_ps, 1)
                elif name == "mT":
                    pe.wait_ge(s_mx, u.n * HEADS + HEADS)
                    bank_free(pe, unit, name)
                    nc.tensor.transpose(ps[0:2 * HEADS, 0:HT],
                                        mx[p2][:, :, :].rearrange("p q h -> p (q h)"), ident[0:HT, 0:HT])\
                      .then_inc(s_mT_ps, 1)
                elif name in ("ot0", "ot1"):
                    h = int(name[2])
                    pe.wait_ge(s_o, u.n * GROUPS + GROUPS)
                    bank_free(pe, unit, name)
                    for g in range(GROUPS):
                        last = nc.tensor.transpose(ps[0:HT, g * 128:g * 128 + 128],
                                                   o_sb[p2][:, g, h * HT:h * HT + HT], ident[:, :])
                    last.then_inc(s_ot_ps, 1)
                elif name == "oT":
                    pe.wait_ge(s_on, u.n * 2 + 2)
                    bank_free(pe, unit, name)
                    for c in range(2):
                        for h in range(2):
                            last = nc.tensor.transpose(ps[0:CC, c * TOK + h * HT:c * TOK + h * HT + HT],
                                                       on[p2][:, h, c * CC:c * CC + CC], ident[0:HT, 0:HT])
                    last.then_inc(s_oT_ps, 1)
                elif name == "y":
                    pe.wait_ge(s_olo, u.n + 1)
                    bank_free(pe, unit, name)
                    o_part = (oT_hi[p2], oT_lo[p2])
                    for h in range(2):
                        split_product(ps[0:HT, h * C:h * C + C],
                                      lambda a, c: o_part[a][:, c, h * HT:h * HT + HT],
                                      lambda b, c: w_part[b][:, lay, c, 3 * C:4 * C],
                                      s_y_ps if h else None)

            def iteration(unit, layer):
                for s in range(HEADS):
                    u = unit(LAG_MAX)
                    if active(u):
                        if s == 0:
                            wait_dma(pe, s_rel, u, 8)
                        wait(pe, s_mx, u.n * HEADS + s - 1)
                        for h in range(2):
                            last = nc.tensor.matmul(ps_max[s % 2][0:HT, h * TOK:h * TOK + TOK],
                                                    q_st[u.r][0:R_MAX, h, s, :], k_st[u.r][0:R_MAX, s, :],
                                                    start=True, stop=True)
                        last.then_inc(s_sm_ps, 1)
                    u, head = c_step(unit, s)
                    if active(u):
                        if head == 0:
                            wait_dma(pe, s_m, u)
                        wait(pe, s_p, u.n * HEADS + head - 1)
                        for kt in range(2):
                            last = nc.tensor.matmul(ps_sc[head % 2][0:HT, kt * TOK:kt * TOK + TOK],
                                                    k_st[u.r][0:STACK, head, kt * HT:kt * HT + HT],
                                                    q_st[u.r][0:STACK, :, head, :],
                                                    start=True, stop=True)
                        last.then_inc(s_sc_ps, 1)
                    for name in JOBS.get(s, ()):
                        job(name, unit, layer)
                    if s in PV_SLOT:
                        lag, g, kt = PV_SLOT[s]
                        u = unit(lag)
                        if active(u):
                            n = u.n * GROUPS + g
                            bank = ps_o[(u.r * GROUPS + g) % 2]
                            if kt == 0:
                                wait(pe, s_v, u.n + 1)
                                wait(pe, s_p, u.n * HEADS + HG * g + HG)
                                wait(pe, s_o, n - 1)
                            for j in range(HG):
                                head = HG * g + j
                                p = probs[(HEADS * u.r + head) % PRING]
                                last = nc.tensor.matmul(bank[32 * j:32 * j + 32, 0:TOK],
                                                        v_st[u.r][:, kt, head, :], p[:, kt, :],
                                                        start=kt == 0, stop=kt == 1)
                            if kt == 1:
                                last.then_inc(s_o_ps, 1)

            run(pe, iteration)

        @block.scalar
        def _(act):
            act.wait_ge(s_setup, 1)

            def iteration(unit, layer):
                for s in range(HEADS):
                    u, head = c_step(unit, s)
                    if active(u):
                        n = u.n * HEADS + head
                        wait(act, s_sc_ps, n + 1)
                        wait(act, s_o_ps, u.n * GROUPS + head // HG - 1)
                        nc.scalar.activation(
                            probs[(HEADS * u.r + head) % PRING][:, :, :],
                            ps_sc[head % 2][0:HT, 0:2 * TOK].rearrange("p (k t) -> p k t", k=2),
                            ACT.Exp, scale=1.0 / (QS * KS)).then_inc(s_p, 1)
                    u = unit(LAG_MT)
                    if s == 1 and active(u):
                        act.wait_ge(s_mT_ps, u.n + 1)
                        b4 = unit(LAG_MT + 2)
                        if active(b4):
                            wait_dma(act, s_m, b4)
                        nc.scalar.activation(mrow[u.r % 2][:, :], ps_m[BANK["mT"]][0:2 * HEADS, 0:HT],
                                             ACT.Copy, scale=-1.0 / KS).then_inc(s_mrow, 1)
                    u = unit(LAG_A)
                    if s == 3 and active(u):
                        act.wait_ge(s_xT_ps, u.n + 1)
                        wait(act, s_xn, u.n * 2 - 2)
                        nc.scalar.copy(xT[u.r % 2][:, :, :],
                                       ps_m[BANK["xT"]][0:CC, 0:2 * TOK].rearrange("p (c t) -> p c t", c=2))\
                          .then_inc(s_xT, 1)
                    u = unit(LAG_REL)
                    for n, at in enumerate((3, 5, 6)):
                        if s == at and active(u):
                            ps = ps_m[BANK[f"rel{n}"]]
                            rows, a0 = RELB[n], sum(RELB[:n])
                            act.wait_ge(s_rel_ps, u.n * 3 + n + 1)
                            b4 = unit(LAG_REL + 2)
                            if n == 0 and active(b4):
                                wait_dma(act, s_rel, b4, 8)
                            for dst, src in rel_views(rel_hi[u.r % 2], ps, rows, a0):
                                nc.scalar.copy(dst, src).then_inc(s_rhi, 1)
                    for slot, (lag, g, kt) in PV_SLOT.items():
                        if kt == 1 and s == (slot + 1) % HEADS:
                            u = unit(lag + (slot + 1) // HEADS)
                            if active(u):
                                act.wait_ge(s_o_ps, u.n * GROUPS + g + 1)
                                wait(act, s_ot_ps, u.n * 2 - 2)
                                nc.scalar.copy(o_sb[u.r % 2][:, g, :],
                                               ps_o[(u.r * GROUPS + g) % 2][:, 0:TOK]).then_inc(s_o, 1)
                    u = unit(LAG_A)
                    if s == 8 and active(u):
                        act.wait_ge(s_xn, u.n * 2 + 2)
                        wait(act, s_v_ps, u.n - 1)
                        nc.scalar.copy(xn_hi[u.r % 2][:, :, :], xn[u.r % 2][:, :, :]).then_inc(s_xhi, 1)
                    for name, at, full, dst, done in (("q", 9, s_q_ps, q_hi, s_qhi), ("k", 10, s_k_ps, k_hi, s_khi)):
                        if s == at and active(u):
                            act.wait_ge(full, u.n + 1)
                            b4 = unit(LAG_A + 2)
                            if active(b4):
                                wait_dma(act, s_qkd, b4, 6)
                            lay = layer_of(u, layer)
                            for m in range(2):
                                t = 2 * (name == "k") + m
                                nc.scalar.activation(dst[u.r % 2][:, m, :],
                                                     ps_m[BANK[name]][0:CC, m * TOK:m * TOK + TOK],
                                                     ACT.Identity, bias=bqk[:, lay, t:t + 1]).then_inc(done, 1)
                    u = unit(LAG_D)
                    if s == 10 and active(u):
                        act.wait_ge(s_oT_ps, u.n + 1)
                        wait(act, s_y_ps, u.n - 1)
                        nc.scalar.copy(oT_hi[u.r % 2][:, :, :],
                                       ps_m[BANK["oT"]][0:CC, 0:2 * TOK].rearrange("p (c t) -> p c t", c=2))\
                          .then_inc(s_ohi, 1)

            run(act, iteration)

        @block.vector
        def _(dve):
            nc.vector.memset(rel_raw[:, :, :, :], 0.0).then_inc(s_pad, 1)
            nc.vector.memset(halfpow[:, :], -0.5)
            nc.vector.memset(eps[:, :], EPS)
            for i in range(UNROLL):
                nc.vector.memset(v_st[i][:, :, :, :], VS)
            dve.wait_ge(s_const, 16 * 6)
            for i in range(UNROLL):
                for head in range(HEADS):
                    nc.vector.tensor_copy(k_st[i][R_REL:STACK, head, :], oh_raw[R_REL:STACK, :])
            nc.vector.tensor_scalar(bqk[:, :, 0:2], bqk_raw[:, :, 0:2], QS, None, ALU.mult)
            nc.vector.tensor_scalar(bqk[:, :, 2:4], bqk_raw[:, :, 2:4], KS * HD ** -0.5, None, ALU.mult)
            nc.vector.tensor_scalar(brow[:, :, 0, :], brow[:, :, 0, :], VS, None, ALU.mult)
            nc.vector.tensor_scalar(rel_raw[:, :, :, :], rel_raw[:, :, :, :], RS, None, ALU.mult)\
              .then_inc(s_wsc, 1)
            dve.wait_ge(s_wsc, 1)
            nc.vector.tensor_copy(rel_st[:, :, :, :], rel_raw[:, :, :, :]).then_inc(s_whi, 1)
            dve.wait_ge(s_whi, 1)
            nc.vector.tensor_tensor(rel_st[32:64, :, :, :], rel_raw[32:64, :, :, :], rel_st[32:64, :, :, :],
                                    ALU.subtract)
            for layer in range(LAYERS):
                dve.wait_ge(s_wraw[layer], 16)
                for lo, hi, f in ((0, C, QS), (C, 2 * C, KS * HD ** -0.5), (2 * C, 4 * C, VS)):
                    nc.vector.tensor_scalar(w_raw[:, :, lo:hi], w_raw[:, :, lo:hi], f, None, ALU.mult)\
                      .then_inc(s_wsc, 1)
                dve.wait_ge(s_wsc, 1 + 3 * (layer + 1))
                nc.vector.tensor_copy(w_hi[:, layer, :, :], w_raw[:, :, :]).then_inc(s_whi, 1)
                dve.wait_ge(s_whi, 2 + layer)
                nc.vector.tensor_tensor(w_lo[:, layer, :, :], w_raw[:, :, :], w_hi[:, layer, :, :],
                                        ALU.subtract).then_inc(s_wlo, 1)
            dve.wait_ge(s_wlo, LAYERS)
            nc.vector.memset(yo[0][:, :, :], 0.0).then_inc(s_setup, 1)

            def iteration(unit, layer):
                for s in range(HEADS):
                    u = unit(LAG_MAX)
                    if active(u):
                        n = u.n * HEADS + s
                        dve.wait_ge(s_sm_ps, n + 1)
                        if s == 0:
                            wait(dve, s_mT_ps, u.n - 1)
                        nc.vector.reduce_max(mx[u.r % 2][:, :, s],
                                             ps_max[s % 2][0:HT, 0:2 * TOK].rearrange("p (q k) -> p q k", q=2),
                                             axis=AX.X).then_inc(s_mx, 1)
                    u = unit(LAG_A)
                    p2 = u.r % 2
                    if s == 4 and active(u):
                        dve.wait_ge(s_xT, u.n + 1)
                        for c in range(2):
                            nc.vector.bn_stats(bn6[p2][:, c, :], xT[p2][:, c, :]).then_inc(s_bn, 1)
                        dve.wait_ge(s_bn, u.n * 2 + 2)
                        wait(dve, s_g_ps, u.n - 1)
                        nc.vector.memset(anchor[:, 0:1], 0.0)
                        for c in range(2):
                            nc.vector.bn_aggr(mv[p2][:, c, :], bn6[p2][:, c, :]).then_inc(s_agg, 1)
                    if s == 5 and active(u):
                        dve.wait_ge(s_g_ps, u.n + 1)
                        wait(dve, s_gp, u.n * 5 - 5)
                        nc.vector.tensor_copy(gsm[p2][:, :, :],
                                              ps_m[BANK["g"]][0:CC, 0:4].rearrange("p (c s) -> p c s", c=2))\
                          .then_inc(s_g, 1)
                    u = unit(LAG_REL)
                    for n, at in enumerate((3, 5, 6)):
                        if s == at and active(u):
                            ps = ps_m[BANK[f"rel{n}"]]
                            rows, a0 = RELB[n], sum(RELB[:n])
                            b4 = unit(LAG_REL + 2)
                            if n == 0 and active(b4):
                                wait_dma(dve, s_rel, b4, 8)
                            hi = rel_views(rel_hi[u.r % 2], ps, rows, a0)
                            lo = rel_views(rel_lo[u.r % 2], ps, rows, a0)
                            dve.wait_ge(s_rhi, u.n * 6 + 2 * n + 2)
                            for (h, src), (l, _) in zip(hi, lo):
                                nc.vector.tensor_tensor(l, src, h, ALU.subtract).then_inc(s_rlo, 1)
                    u = unit(LAG_D)
                    p2 = u.r % 2
                    for h, at in ((0, 8), (1, 9)):
                        if s == at and active(u):
                            ps = ps_m[BANK[f"ot{h}"]][0:HT, 0:HEADS * PW].rearrange("p (h d) -> p h d", d=PW)
                            dve.wait_ge(s_ot_ps, u.n * 2 + h + 1)
                            nc.vector.reciprocal(rsum[p2][:, h, :], ps[:, :, HD]).then_inc(s_rs, 1)
                            dve.wait_ge(s_rs, u.n * 2 + h + 1)
                            wait(dve, s_oT_ps, u.n - 1)
                            nc.vector.tensor_tensor(
                                on[p2][:, h, :].rearrange("p (h d) -> p h d", d=HD), ps[:, :, 0:HD],
                                rsum[p2][:, h, :].rearrange("p (h o) -> p h o", o=1).to_broadcast([HT, HEADS, HD]),
                                ALU.mult).then_inc(s_on, 1)
                    if s == 10 and active(u):
                        dve.wait_ge(s_ohi, u.n + 1)
                        wait(dve, s_y_ps, u.n - 1)
                        nc.vector.tensor_tensor(oT_lo[p2][:, :, :],
                                                ps_m[BANK["oT"]][0:CC, 0:2 * TOK].rearrange("p (c t) -> p c t", c=2),
                                                oT_hi[p2][:, :, :], ALU.subtract).then_inc(s_olo, 1)
                    u = unit(LAG_A)
                    lay = layer_of(u, layer)
                    for name, at, hi, lo, hi_done, lo_done in (("q", 9, q_hi, q_lo, s_qhi, s_qlo),
                                                               ("k", 10, k_hi, k_lo, s_khi, s_klo)):
                        if s == at and active(u):
                            dve.wait_ge(hi_done, u.n * 2 + 2)
                            b4 = unit(LAG_A + 2)
                            if active(b4):
                                wait_dma(dve, s_qkd, b4, 6)
                            for m in range(2):
                                t = 2 * (name == "k") + m
                                nc.vector.scalar_tensor_tensor(
                                    out=lo[u.r % 2][:, m, :], in0=ps_m[BANK[name]][0:CC, m * TOK:m * TOK + TOK],
                                    scalar=bqk[:, lay, t:t + 1], in1=hi[u.r % 2][:, m, :],
                                    op0=ALU.add, op1=ALU.subtract).then_inc(lo_done, 1)
                    if s == 11 and active(u):
                        dve.wait_ge(s_v_ps, u.n + 1)
                        wait(dve, s_o_ps, (u.n - 3) * GROUPS)
                        for h in range(2):
                            last = nc.vector.tensor_tensor(
                                v_st[u.r][:, h, :, 0:HD],
                                ps_m[BANK["v"]][0:HT, h * C:h * C + C].rearrange("p (h d) -> p h d", d=HD),
                                brow[:, lay, 0, :].rearrange("p (h d) -> p h d", d=HD), ALU.add)
                        last.then_inc(s_v, 1)
                    u = unit(LAG_D)
                    if s == 11 and active(u):
                        dve.wait_ge(s_y_ps, u.n + 1)
                        dve.wait_ge(s_xb, u.n + 1)
                        b4 = unit(LAG_D + 2)
                        if active(b4):
                            wait_dma(dve, s_out, b4)
                        nc.vector.scalar_tensor_tensor(
                            out=yo[p2][:, :, :],
                            in0=ps_m[BANK["y"]][0:HT, 0:2 * C].rearrange("p (h c) -> p h c", h=2),
                            scalar=1.0 / VS, in1=xb[p2][:, :, :], op0=ALU.mult, op1=ALU.add).then_inc(s_y, 1)

            run(dve, iteration)

        @block.gpsimd
        def _(pool):
            pool.wait_ge(s_setup, 1)

            def iteration(unit, layer):
                d = unit(LAG_D)
                if active(d):
                    lay = layer_of(d, layer)
                    wait_dma(pool, s_xd, d)
                    wait(pool, s_y, d.n - 1)
                    for h in range(2):
                        last = nc.gpsimd.tensor_tensor(xb[d.r % 2][:, h, :], xd[d.r % 2][:, h, :],
                                                       brow[:, lay, 1, :], ALU.add)
                    last.then_inc(s_xb, 1)
                u = unit(LAG_A)
                if active(u):
                    p2 = u.r % 2
                    pool.wait_ge(s_agg, u.n * 2 + 2)
                    nc.gpsimd.tensor_tensor(msq[p2][:, :], mv[p2][:, :, 0], mv[p2][:, :, 0], ALU.mult)\
                      .then_inc(s_sq, 1)
                    pool.wait_ge(s_sq, u.n + 1)
                    nc.gpsimd.tensor_tensor(mv[p2][:, :, 1], mv[p2][:, :, 1], msq[p2][:, :], ALU.add)\
                      .then_inc(s_mv, 1)
                    pool.wait_ge(s_g, u.n + 1)
                    nc.gpsimd.tensor_tensor(msq[p2][:, :], gsm[p2][:, :, 0], gsm[p2][:, :, 0], ALU.mult)\
                      .then_inc(s_gp, 1)
                    pool.wait_ge(s_gp, u.n * 5 + 1)
                    nc.gpsimd.tensor_tensor(gvar[p2][:, :], gsm[p2][:, :, 1], msq[p2][:, :], ALU.subtract)\
                      .then_inc(s_gp, 1)
                    pool.wait_ge(s_gp, u.n * 5 + 2)
                    nc.gpsimd.tensor_tensor(gvar[p2][:, :], gvar[p2][:, :], eps[:, :], ALU.add)\
                      .then_inc(s_gp, 1)
                    pool.wait_ge(s_gp, u.n * 5 + 3)
                    nc.gpsimd.tensor_tensor(rstd[p2][:, :], gvar[p2][:, :], halfpow[:, :], ALU.pow)\
                      .then_inc(s_gp, 1)
                    nc.gpsimd.tensor_scalar(nmean[p2][:, :], gsm[p2][:, :, 0], -1.0, None, ALU.mult)\
                      .then_inc(s_gp, 1)
                    pool.wait_ge(s_gp, u.n * 5 + 5)
                    nc.gpsimd.tensor_tensor(anchor[:, 1:3], eps[:, :], eps[:, :], ALU.add)
                    for c in range(2):
                        nc.gpsimd.tensor_scalar(xn[p2][:, c, :], xT[p2][:, c, :], nmean[p2][:, c:c + 1],
                                                rstd[p2][:, c:c + 1], ALU.add, ALU.mult).then_inc(s_xn, 1)
                    pool.wait_ge(s_xhi, u.n + 1)
                    nc.gpsimd.tensor_tensor(xn_lo[p2][:, :, :], xn[p2][:, :, :], xn_hi[p2][:, :, :],
                                            ALU.subtract).then_inc(s_xlo, 1)

            run(pool, iteration)


def kernel(x, L0_conv_qkv_w, L0_conv_qkv_b, L0_conv_rel_pos_h, L0_conv_rel_pos_w, L0_conv_proj_w,
           L0_conv_proj_b, L1_conv_qkv_w, L1_conv_qkv_b, L1_conv_proj_w, L1_conv_proj_b,
           L1_conv_rel_pos_h, L1_conv_rel_pos_w):
    import numpy as np
    import concourse.bacc as bacc
    from concourse.bass_utils import run_bass_kernel_spmd

    def a(v):
        return np.asarray(v)

    perm = (np.arange(2)[:, None, None] * CC + np.arange(HC)[None, None, :] * HD
            + np.arange(HD)[None, :, None]).reshape(-1)

    def weights(qkv, proj):
        return np.concatenate([qkv[:, perm], qkv[:, C + perm], qkv[:, 2 * C:], proj], axis=1)

    w_all = np.stack([weights(a(L0_conv_qkv_w).T, a(L0_conv_proj_w).T),
                      weights(a(L1_conv_qkv_w), a(L1_conv_proj_w))])
    qkv_b = [a(L0_conv_qkv_b), a(L1_conv_qkv_b)]
    proj_b = [a(L0_conv_proj_b), a(L1_conv_proj_b)]
    b_qk = np.stack([np.concatenate([b[perm], b[C + perm]]).reshape(4, CC).T for b in qkv_b], axis=1)
    b_rows = np.stack([np.stack([b[2 * C:], p]) for b, p in zip(qkv_b, proj_b)])
    b_rows = np.broadcast_to(b_rows[None], (HT, LAYERS, 2, C))
    rel = np.stack([np.stack([a(h)[REL - 1::-1].T, a(w)[REL - 1::-1].T], axis=1) for h, w in
                    ((L0_conv_rel_pos_h, L0_conv_rel_pos_w), (L1_conv_rel_pos_h, L1_conv_rel_pos_w))], axis=1)
    rel = np.concatenate([rel] * 4, axis=0)

    rows = np.arange(TOK) // SIDE == np.arange(SIDE)[:, None]
    cols = np.arange(TOK) % SIDE == np.arange(SIDE)[:, None]
    onehot = np.concatenate([KS / RS * np.concatenate([rows, cols] * 2), np.full((1, TOK), KS)]).astype(np.float32)
    ident = np.eye(128, dtype=np.float32)
    group = np.arange(CC) // GROUP
    gmat = ((group[:, None] == group[None, :]) / GROUP).astype(np.float32)

    ins = {"x": a(x).reshape(SAMPLES, TOK, C), "w_all": w_all, "b_qk": b_qk, "b_rows": b_rows, "rel": rel,
           "onehot": onehot, "ident": ident, "gmat": gmat}
    ins = {k: np.ascontiguousarray(v) for k, v in ins.items()}
    nc = bacc.Bacc("TRN2", target_bir_lowering=False, num_devices=1)
    args = [nc.dram_tensor(f"in_{k}", v.shape, mybir.dt.from_np(v.dtype), kind="ExternalInput").ap()
            for k, v in ins.items()]
    args.append(nc.dram_tensor("out_0", (SAMPLES, TOK, C), F32, kind="ExternalOutput").ap())
    attention_kernel(nc, *args)
    r = run_bass_kernel_spmd(nc, [{f"in_{k}": v for k, v in ins.items()}], core_ids=[0])
    return r.results[0]["out_0"].reshape(SAMPLES, SIDE, SIDE, C)
```

```python
from contextlib import ExitStack

import concourse.bass as bass
from concourse import mybir

F32 = mybir.dt.float32
F16 = mybir.dt.float16
ALU = mybir.AluOpType
ACT = mybir.ActivationFunctionType
AX = mybir.AxisListType

LAYERS = 2
SAMPLES = 64
UNITS = LAYERS * SAMPLES
SIDE = 14
TOK = SIDE * SIDE
HT = TOK // 2
HALF = SIDE // 2
C = 192
CC = C // 2
HEADS = 12
HD = C // HEADS
HQ = 64 // HD
NT = HEADS // HQ
HH = HEADS // 2
GROUP = C // 32
EPS = 1e-5
REL = 2 * SIDE - 1

QS = 32.0
KS = 32.0
RS = 4.0
VS = 32.0

RW = 32
R_REL = 4 * HD
R_MAX = R_REL + RW + 2 * SIDE
STACK = R_MAX + 1

PW = 32
HG = 4
GROUPS = HEADS // HG
RELB = (6, 6, 2)
RP = 2 * (SIDE - 1) + RW
UNROLL = 4


class Unit:

    def __init__(self, block, place):
        self.block = block + place // UNROLL
        self.r = place % UNROLL
        self.n = self.block * UNROLL + self.r
        self.fixed = isinstance(block, int)


def attention_kernel(nc, x, w_all, b_qk, b_rows, rel, onehot, lo_rows, ident_in, gmat_in, out):
    with ExitStack() as ctx:
        def sb(name, shape, dt=F32):
            return ctx.enter_context(nc.sbuf_tensor(name, shape, dt))

        def psum(name, shape):
            return ctx.enter_context(nc.psum_tensor(name, shape, F32))

        def sem(name):
            return ctx.enter_context(nc.semaphore(name))

        def sems(name, n=UNROLL):
            return [sem(f"{name}{i}") for i in range(n)]

        x1 = nc.dram_tensor("x1", [SAMPLES, TOK, C], F32).ap()
        q_dram = nc.dram_tensor("q_dram", [UNROLL, 2, HD, HQ, NT, TOK], F16).ap()
        k_dram = nc.dram_tensor("k_dram", [UNROLL, 2, HD, HQ, NT, TOK], F16).ap()

        ident = sb("ident", [128, 128])
        gmat = sb("gmat", [CC, CC])
        w_raw = sb("w_raw", [CC, 2, 4 * C])
        w_hi = sb("w_hi", [CC, LAYERS, 2, 4 * C], F16)
        w_lo = sb("w_lo", [CC, LAYERS, 2, 4 * C], F16)
        bqk_raw = sb("bqk_raw", [128, LAYERS, NT])
        bqk = sb("bqk", [128, LAYERS, NT])
        brow = sb("brow", [HT, LAYERS, 2, C])
        rel_raw = sb("rel_raw", [64, LAYERS, 2, RP])
        rel_st = sb("rel_st", [64, LAYERS, 2, RP], F16)
        oh_raw = sb("oh_raw", [128, TOK])
        is_lo = sb("is_lo", [128, 1])
        halfpow = sb("halfpow", [CC, 2])
        eps = sb("eps", [CC, 2])
        anchor = sb("anchor", [CC, 3])

        q_st = [sb(f"q_st{i}", [128, HEADS, 2, HT], F16) for i in range(4)]
        k_st = [sb(f"k_st{i}", [128, HEADS, TOK], F16) for i in range(4)]
        v_st = [sb(f"v_st{i}", [HT, 2, HEADS, PW]) for i in range(4)]

        def pair(name, shape, dt=F32):
            return [sb(f"{name}{i}", shape, dt) for i in range(2)]

        xa = pair("xa", [HT, 2, C])
        xT = pair("xT", [CC, 2, TOK])
        bn6 = pair("bn6", [CC, 2, 6])
        mv = pair("mv", [CC, 2, 2])
        gsm = pair("gsm", [CC, 2, 2])
        msq = pair("msq", [CC, 2])
        gvar = pair("gvar", [CC, 2])
        rstd = pair("rstd", [CC, 2])
        nmean = pair("nmean", [CC, 2])
        xn = pair("xn", [CC, 2, TOK])
        xn_hi = pair("xn_hi", [CC, 2, TOK], F16)
        xn_lo = pair("xn_lo", [CC, 2, TOK], F16)
        qk_hl = pair("qk_hl", [128, 2, NT, TOK], F16)
        rel_hi = pair("rel_hi", [128, HH, TOK], F16)
        rel_hl = pair("rel_hl", [128, HH, TOK], F16)
        mx = pair("mx", [HT, HEADS, 2])
        mrow = pair("mrow", [HEADS, 2, HT], F16)
        probs = [sb(f"probs{i}", [HT, 2, TOK]) for i in range(HEADS)]
        o_sb = pair("o_sb", [128, GROUPS, TOK])
        rsum = pair("rsum", [HT, 2 * HEADS])
        on = pair("on", [HT, 2, C])
        oT_hi = pair("oT_hi", [CC, 2, TOK], F16)
        oT_lo = pair("oT_lo", [CC, 2, TOK], F16)
        xd = pair("xd", [HT, 2, C])
        xb = pair("xb", [HT, 2, C])
        yo = pair("yo", [HT, 2, C])

        ps_max = [psum(f"ps_max{i}", [128, 512]) for i in range(2)]
        ps_sc = [psum(f"ps_sc{i}", [128, 512]) for i in range(2)]
        ps_o = psum("ps_o", [128, 512])
        ps_m = [psum(f"ps_m{i}", [128, 512]) for i in range(3)]

        s_const = sem("s_const")
        s_wraw = sems("s_wraw", 2)
        s_pad = sem("s_pad")
        s_wsc = sem("s_wsc")
        s_whi = sem("s_whi")
        s_wlo = sem("s_wlo")
        s_setup = sem("s_setup")
        s_x = sems("s_x")
        s_xT_ps = sem("s_xT_ps")
        s_xT = sem("s_xT")
        s_bn = sem("s_bn")
        s_agg = sem("s_agg")
        s_sq = sem("s_sq")
        s_mv = sem("s_mv")
        s_g_ps = sem("s_g_ps")
        s_g = sem("s_g")
        s_gp = sem("s_gp")
        s_xn = sem("s_xn")
        s_xhi = sem("s_xhi")
        s_xlo = sem("s_xlo")
        s_qk_ps = sem("s_qk_ps")
        s_v_ps = sem("s_v_ps")
        s_qkhi = sem("s_qkhi")
        s_qklo = sem("s_qklo")
        s_v = sem("s_v")
        s_qd = sems("s_qd")
        s_kd = sems("s_kd")
        s_qst = sems("s_qst")
        s_kst = sems("s_kst")
        s_rel_ps = sem("s_rel_ps")
        s_rhi = sem("s_rhi")
        s_rlo = sem("s_rlo")
        s_rel = sems("s_rel")
        s_sm_ps = sem("s_sm_ps")
        s_mx = sem("s_mx")
        s_mT_ps = sem("s_mT_ps")
        s_mrow = sem("s_mrow")
        s_m = [sems(f"s_m{h}_") for h in range(2)]
        s_sc_ps = sem("s_sc_ps")
        s_p = sem("s_p")
        s_o_ps = sem("s_o_ps")
        s_o = sem("s_o")
        s_ot_ps = sem("s_ot_ps")
        s_rs = sem("s_rs")
        s_on = sem("s_on")
        s_oT_ps = sem("s_oT_ps")
        s_ohi = sem("s_ohi")
        s_olo = sem("s_olo")
        s_y_ps = sem("s_y_ps")
        s_xd = sems("s_xd")
        s_xb = sem("s_xb")
        s_y = sem("s_y")
        s_out = sems("s_out")

        block = ctx.enter_context(nc.Block())

        def wait(eng, s, value):
            if not (isinstance(value, int) and value <= 0):
                eng.wait_ge(s, value)

        def wait_dma(eng, group, u, dmas=1):
            wait(eng, group[u.r], (u.block + 1) * (16 * dmas))

        def head_of(place):
            return place % NT * HQ + place // NT

        def active(u):
            return not u.fixed or 0 <= u.n < UNITS

        def layer_of(u, loop_layer):
            return loop_layer if not u.fixed else u.n // SAMPLES

        def run(eng, iteration):
            at = -1
            for layer in range(LAYERS):
                first = layer * SAMPLES
                start = first + UNROLL * (2 if layer == 0 else 1)
                stop = first + SAMPLES - UNROLL
                for i in range(at, start):
                    iteration(lambda lag, i=i: Unit(0, i - lag), layer)
                with eng.Fori(start // UNROLL, stop // UNROLL) as t:
                    eng.compute_val(t * UNROLL)
                    for r in range(UNROLL):
                        iteration(lambda lag, t=t, r=r: Unit(t, r - lag), layer)
                at = stop
            for i in range(at, UNITS + UNROLL):
                iteration(lambda lag, i=i: Unit(0, i - lag), LAYERS - 1)

        MAX_AT, EXP_AT = 2 * HEADS, 3 * HEADS
        PV_AT = {(0, 0): 41, (0, 1): 44, (1, 0): 46, (1, 1): 49, (2, 0): 50, (2, 1): 51}
        O_LATER = 1

        JOBS = [(12, "v0", 2, (s_v, 2, 1)),
                (13, "rel0", 0, (s_rlo, 6, 2)), (13, "v1", 2, (s_v, 2, 2)),
                (14, "rel1", 2, (s_rlo, 6, 4)),
                (15, "rel2", 1, (s_rlo, 6, 6)), (39, "mT1", 0, (s_mrow, 2, 2)),
                (4, "qk0", 0, (s_qklo, NT, 1)), (4, "qk1", 2, (s_qklo, NT, 2)),
                (5, "qk2", 1, (s_qklo, NT, 3)), (53, "ot", 0, (s_on, 1, 1)),
                (30, "mT0", 2, (s_mrow, 2, 1)), (54, "oT", 0, (s_olo, 1, 1)),
                (-5, "xT", 1, (s_xT, 1, 1)),
                (57, "y", 1, (s_y, 1, 1)), (-3, "g", 0, (s_g, 1, 1))]
        ORDER = [name for _, name, _, _ in JOBS]
        AT = {name: at for at, name, _, _ in JOBS}
        BANK = {name: bank for _, name, bank, _ in JOBS}
        READ = {name: read for _, name, _, read in JOBS}
        BN_AT, XHI_AT = AT["xT"], 2
        REL_LO_LATER = 1

        LAG_X, LAG_A, LAG_REL, LAG_MAX, LAG_C, LAG_D = -1, 0, 1, 2, 3, 4

        def due(unit, slot, at):
            u = unit(at // HEADS)
            return u if at % HEADS == slot and active(u) else None

        def bank_free(pe, unit, job):
            at = ORDER.index(job)
            for back in range(1, 6 * len(ORDER)):
                turns, k = divmod(at - back, len(ORDER))
                u = unit(AT[ORDER[k]] // HEADS - turns)
                if BANK[ORDER[k]] == BANK[job] and active(u):
                    s, per, which = READ[ORDER[k]]
                    wait(pe, s, u.n * per + which)
                    return

        def rel_views(dst, ps, n, a0):
            by_row = (dst[0:64, :, a0 * SIDE:(a0 + n) * SIDE].rearrange("p h (a b) -> p a h b", a=n),
                      ps[0:64, 0:n * HH * SIDE].rearrange("p (a h b) -> p a h b", a=n, h=HH))
            by_col = (dst[64:128, :, :].rearrange("p h (a b) -> p b h a", a=SIDE)[:, a0:a0 + n],
                      ps[64:128, 0:n * HH * SIDE].rearrange("p (b h a) -> p b h a", b=n, h=HH))
            return by_row, by_col

        @block.sync
        def _(sp):
            sp.dma_start(ident[:, :], ident_in).then_inc(s_const, 16)
            sp.dma_start(gmat[:, :], gmat_in).then_inc(s_const, 16)
            sp.dma_start(oh_raw[R_REL:STACK, :], onehot).then_inc(s_const, 16)
            sp.dma_start(is_lo[:, :], lo_rows).then_inc(s_const, 16)
            sp.dma_start(bqk_raw[:, :, :], b_qk).then_inc(s_const, 16)
            sp.dma_start(brow[:, :, :, :], b_rows).then_inc(s_const, 16)
            sp.wait_ge(s_pad, 1)
            sp.dma_start(rel_raw[:, :, :, 0:2 * REL], rel).then_inc(s_const, 16)
            for layer in range(LAYERS):
                if layer:
                    sp.wait_ge(s_wlo, layer)
                sp.dma_start(w_raw[:, :, :], w_all[layer].rearrange("(c p) n -> p c n", c=2))\
                  .then_inc(s_wraw[layer], 16)

            def tokens(dram):
                return dram.rearrange("o (h t) c -> t (o h) c", h=2)

            def iteration(unit, layer):
                n, u, e, m, c, d = (unit(lag) for lag in (LAG_X, LAG_A, LAG_REL, LAG_MAX, LAG_C, LAG_D))
                if active(n) and not n.fixed:
                    for value in (n.n, n.n - 1):
                        sp.compute_val(value)
                if active(n):
                    nl = layer_of(n, layer)
                    if nl:
                        wait_dma(sp, s_out, unit(LAG_X + SAMPLES))
                    src, at = (x, n.n) if not nl else (x1, n.n - SAMPLES)
                    wait(sp, s_xT_ps, n.n - 1)
                    sp.dma_start(xa[n.r % 2][:, :, :], tokens(src[bass.ds(at, 1)])).then_inc(s_x[n.r], 16)
                dl = layer_of(d, layer)
                if active(d):
                    src, at = (x, d.n) if not dl else (x1, d.n - SAMPLES)
                    wait(sp, s_xb, d.n - 1)
                    sp.dma_start(xd[d.r % 2][:, :, :], tokens(src[bass.ds(at, 1)])).then_inc(s_xd[d.r], 16)
                def maxima(unit_, half):
                    if active(unit_):
                        wait(sp, s_mrow, unit_.n * 2 + half + 1)
                        sp.dma_start(q_st[unit_.r][R_MAX:STACK, half * HH:half * HH + HH, :, :],
                                     mrow[unit_.r % 2][:, half, :]).then_inc(s_m[half][unit_.r], 16)

                def to_dram(unit_, dram, row, landed):
                    sp.dma_start(dram[unit_.r].rearrange("l d h c t -> (d h) l (c t)"),
                                 qk_hl[unit_.r % 2][row:row + HQ * HD, :, :, :]
                                 .rearrange("p l c t -> p l (c t)")).then_inc(landed[unit_.r], 16)

                maxima(c, 1)
                if active(e):
                    wait(sp, s_rlo, e.n * 6 + 6)
                    for axis in range(2):
                        rows = RW if axis == 0 else 2 * SIDE
                        for half in range(2):
                            p, r0 = 64 * axis + 32 * half, R_REL + RW * axis
                            sp.dma_start(q_st[e.r][r0:r0 + rows, half * HH:half * HH + HH, :, :],
                                         rel_hl[e.r % 2][p:p + rows, :, :]).then_inc(s_rel[e.r], 16)
                if active(u):
                    wait(sp, s_qklo, u.n * NT + NT)
                    to_dram(u, q_dram, 0, s_qd)
                maxima(m, 0)
                if active(u):
                    to_dram(u, k_dram, HQ * HD, s_kd)
                    wait_dma(sp, s_qd, u)
                    both = q_dram[u.r:u.r + 1].rearrange("o l d h c t -> o (l d) (h c t)")
                    sp.dma_start(q_st[u.r][0:R_REL, :, :, :],
                                 both.to_broadcast([2, 2 * HD, HEADS * TOK])).then_inc(s_qst[u.r], 16)
                if active(u):
                    wait_dma(sp, s_kd, u)
                    for part in range(2):
                        one = k_dram[u.r, part:part + 1].rearrange("l d h c t -> l d (h c t)")
                        sp.dma_start(k_st[u.r][2 * HD * part:2 * HD * part + 2 * HD, :, :],
                                     one.to_broadcast([2, HD, HEADS * TOK])).then_inc(s_kst[u.r], 16)
                if active(d):
                    wait(sp, s_y, d.n + 1)
                    dst, at = (x1, d.n) if not dl else (out, d.n - SAMPLES)
                    sp.dma_start(tokens(dst[bass.ds(at, 1)]), yo[d.r % 2][:, :, :]).then_inc(s_out[d.r], 16)

            run(sp, iteration)
            for r in range(UNROLL):
                sp.wait_ge(s_out[r], 16 * UNITS // UNROLL)

        @block.tensor
        def _(pe):
            pe.wait_ge(s_setup, 1)
            pe.wait_ge(s_const, 16 * 7)

            def split_product(dst, weights, moving, signal):
                terms = [(a, b, c) for c in range(2) for a, b in ((0, 0), (0, 1), (1, 0))]
                for n, (a, b, c) in enumerate(terms):
                    last = nc.tensor.matmul(dst, weights(a, c), moving(b, c),
                                            start=n == 0, stop=n == len(terms) - 1)
                if signal is not None:
                    last.then_inc(signal, 1)

            def job(name, unit, slot, layer):
                u = due(unit, slot, AT[name])
                if not u:
                    return
                lay = layer_of(u, layer)
                ps, p2 = ps_m[BANK[name]], u.r % 2
                w_part, x_part = (w_hi, w_lo), (xn_hi[p2], xn_lo[p2])
                if name == "xT":
                    wait_dma(pe, s_x, u)
                    bank_free(pe, unit, name)
                    for c in range(2):
                        for h in range(2):
                            last = nc.tensor.transpose(ps[0:CC, c * TOK + h * HT:c * TOK + h * HT + HT],
                                                       xa[p2][:, h, c * CC:c * CC + CC], ident[0:HT, 0:HT])
                    last.then_inc(s_xT_ps, 1)
                elif name == "g":
                    pe.wait_ge(s_mv, u.n + 1)
                    bank_free(pe, unit, name)
                    nc.tensor.matmul(ps[0:CC, 0:4], gmat[:, :], mv[p2][:, :, :], start=True, stop=True)\
                      .then_inc(s_g_ps, 1)
                elif name.startswith("qk"):
                    n0 = int(name[2]) * 128
                    pe.wait_ge(s_xlo, u.n + 1)
                    bank_free(pe, unit, name)
                    split_product(ps[:, 0:TOK], lambda a, c: w_part[a][:, lay, c, n0:n0 + 128],
                                  lambda b, c: x_part[b][:, c, :], s_qk_ps)
                elif name in ("v0", "v1"):
                    h = int(name[1])
                    pe.wait_ge(s_xlo, u.n + 1)
                    bank_free(pe, unit, name)
                    split_product(ps[0:HT, 0:C], lambda a, c: x_part[a][:, c, h * HT:h * HT + HT],
                                  lambda b, c: w_part[b][:, lay, c, 2 * C:3 * C], s_v_ps)
                elif name.startswith("rel"):
                    n = int(name[3])
                    rows = RELB[n]
                    if n == 0:
                        wait_dma(pe, s_qst, u)
                    bank_free(pe, unit, name)
                    nc.tensor.matmul(ps[0:CC, 511:512], w_hi[:, 0, 0, 0:CC], w_hi[:, 0, 0, 0:1],
                                     start=True, stop=True)
                    for i in range(rows):
                        at, a = i * HH * SIDE, sum(RELB[:n]) + i
                        for axis in range(2):
                            w = 2 * (SIDE - 1 - a)
                            for half in range(2):
                                q = q_st[u.r][0:R_REL, half * HH:half * HH + HH, :, :]\
                                    .rearrange("p h q t -> p h (q t)")
                                p = 64 * axis + 32 * half
                                last = nc.tensor.matmul(
                                    ps[p:p + RW, at:at + HH * SIDE], rel_st[:, lay, axis, w:w + RW],
                                    q[:, :, a * SIDE:a * SIDE + SIDE] if axis == 0 else q[:, :, a::SIDE],
                                    start=True, stop=True)
                    last.then_inc(s_rel_ps, 1)
                elif name.startswith("mT"):
                    half = int(name[2])
                    pe.wait_ge(s_mx, u.n * HEADS + HH * (half + 1))
                    bank_free(pe, unit, name)
                    nc.tensor.transpose(ps[0:HEADS, 0:HT],
                                        mx[p2][:, HH * half:HH * half + HH, :].rearrange("p h q -> p (h q)"),
                                        ident[0:HT, 0:HT])\
                      .then_inc(s_mT_ps, 1)
                elif name == "ot":
                    pe.wait_ge(s_o, u.n * GROUPS + GROUPS)
                    bank_free(pe, unit, name)
                    for h in range(2):
                        for g in range(GROUPS):
                            at = (h * GROUPS + g) * HG * (HD + 1)
                            last = nc.tensor.matmul(
                                ps[0:HT, at:at + HG * (HD + 1)], o_sb[p2][:, g, h * HT:h * HT + HT],
                                ident[:, :].rearrange("p (j x) -> p j x", x=PW)[:, :, 0:HD + 1],
                                start=True, stop=True)
                    last.then_inc(s_ot_ps, 1)
                elif name == "oT":
                    pe.wait_ge(s_on, u.n + 1)
                    bank_free(pe, unit, name)
                    for c in range(2):
                        for h in range(2):
                            last = nc.tensor.transpose(ps[0:CC, c * TOK + h * HT:c * TOK + h * HT + HT],
                                                       on[p2][:, h, c * CC:c * CC + CC], ident[0:HT, 0:HT])
                    last.then_inc(s_oT_ps, 1)
                elif name == "y":
                    pe.wait_ge(s_olo, u.n + 1)
                    bank_free(pe, unit, name)
                    o_part = (oT_hi[p2], oT_lo[p2])
                    for h in range(2):
                        split_product(ps[0:HT, h * C:h * C + C],
                                      lambda a, c: o_part[a][:, c, h * HT:h * HT + HT],
                                      lambda b, c: w_part[b][:, lay, c, 3 * C:4 * C],
                                      s_y_ps if h else None)

            def iteration(unit, layer):
                for s in range(HEADS):
                    u = due(unit, s, MAX_AT + s)
                    if u:
                        if s == 0:
                            wait_dma(pe, s_rel, u, 4)
                            wait_dma(pe, s_kst, u, 2)
                        wait(pe, s_mx, u.n * HEADS + s - 1)
                        for h in range(2):
                            last = nc.tensor.matmul(ps_max[s % 2][0:HT, h * TOK:h * TOK + TOK],
                                                    q_st[u.r][0:R_MAX, s, h, :],
                                                    k_st[u.r][0:R_MAX, s, :],
                                                    start=True, stop=True)
                        last.then_inc(s_sm_ps, 1)
                    u, head = due(unit, s, EXP_AT + s), s
                    if u:
                        if head % HH == 0:
                            wait_dma(pe, s_m[head // HH], u)
                        wait(pe, s_p, u.n * HEADS + head - 1)
                        for kt in range(2):
                            last = nc.tensor.matmul(ps_sc[head % 2][0:HT, kt * TOK:kt * TOK + TOK],
                                                    k_st[u.r][0:STACK, head, kt * HT:kt * HT + HT],
                                                    q_st[u.r][0:STACK, head, :, :],
                                                    start=True, stop=True)
                        last.then_inc(s_sc_ps, 1)
                    for name in ORDER:
                        job(name, unit, s, layer)
                    for (g, kt), at in PV_AT.items():
                        u = due(unit, s, at)
                        if u:
                            n = u.n * GROUPS + g
                            if kt == 0:
                                wait(pe, s_v, u.n * 2 + 2)
                                wait(pe, s_p, u.n * HEADS + HG * g + HG)
                                wait(pe, s_o, n)
                            for j in range(HG):
                                head = HG * g + j
                                p = probs[head]
                                last = nc.tensor.matmul(ps_o[32 * j:32 * j + 32, 0:TOK],
                                                        v_st[u.r][:, kt, head_of(head), :], p[:, kt, :],
                                                        start=kt == 0, stop=kt == 1)
                            if kt == 1:
                                last.then_inc(s_o_ps, 1)

            run(pe, iteration)

        @block.scalar
        def _(act):
            act.wait_ge(s_setup, 1)

            def iteration(unit, layer):
                for s in range(HEADS):
                    for g in range(GROUPS):
                        u = due(unit, s, PV_AT[g, 1] + O_LATER)
                        if u:
                            act.wait_ge(s_o_ps, u.n * GROUPS + g + 1)
                            wait(act, s_ot_ps, u.n - 1)
                            nc.scalar.copy(o_sb[u.r % 2][:, g, :], ps_o[:, 0:TOK]).then_inc(s_o, 1)
                    u, head = due(unit, s, EXP_AT + s), s
                    if u:
                        n = u.n * HEADS + head
                        wait(act, s_sc_ps, n + 1)
                        wait(act, s_o_ps, u.n * GROUPS + head // HG - 2)
                        nc.scalar.activation(
                            probs[head][:, :, :],
                            ps_sc[head % 2][0:HT, 0:2 * TOK].rearrange("p (k t) -> p k t", k=2),
                            ACT.Exp, scale=1.0 / (QS * KS)).then_inc(s_p, 1)
                    for half in range(2):
                        name = f"mT{half}"
                        u = due(unit, s, AT[name])
                        if u:
                            act.wait_ge(s_mT_ps, u.n * 2 + half + 1)
                            before = unit(AT[name] // HEADS + 2)
                            if active(before):
                                wait_dma(act, s_m[half], before)
                            nc.scalar.activation(mrow[u.r % 2][:, half, :], ps_m[BANK[name]][0:HEADS, 0:HT],
                                                 ACT.Copy, scale=-1.0 / KS).then_inc(s_mrow, 1)
                    u = due(unit, s, AT["oT"])
                    if u:
                        act.wait_ge(s_oT_ps, u.n + 1)
                        wait(act, s_y_ps, u.n - 1)
                        nc.scalar.copy(oT_hi[u.r % 2][:, :, :],
                                       ps_m[BANK["oT"]][0:CC, 0:2 * TOK].rearrange("p (c t) -> p c t", c=2))\
                          .then_inc(s_ohi, 1)
                    u = due(unit, s, AT["xT"])
                    if u:
                        act.wait_ge(s_xT_ps, u.n + 1)
                        wait(act, s_xn, u.n * 2 - 2)
                        nc.scalar.copy(xT[u.r % 2][:, :, :],
                                       ps_m[BANK["xT"]][0:CC, 0:2 * TOK].rearrange("p (c t) -> p c t", c=2))\
                          .then_inc(s_xT, 1)
                    u = due(unit, s, XHI_AT)
                    if u:
                        act.wait_ge(s_xn, u.n * 2 + 2)
                        wait(act, s_v_ps, u.n * 2 - 2)
                        nc.scalar.copy(xn_hi[u.r % 2][:, :, :], xn[u.r % 2][:, :, :]).then_inc(s_xhi, 1)
                    for n in range(len(RELB)):
                        u = due(unit, s, AT[f"rel{n}"])
                        if u:
                            ps = ps_m[BANK[f"rel{n}"]]
                            rows, a0 = RELB[n], sum(RELB[:n])
                            act.wait_ge(s_rel_ps, u.n * 3 + n + 1)
                            b4 = unit(AT["rel0"] // HEADS + 2)
                            if n == 0 and active(b4):
                                wait_dma(act, s_rel, b4, 4)
                            for axis, (dst, src) in enumerate(rel_views(rel_hi[u.r % 2], ps, rows, a0)):
                                nc.scalar.activation(dst, src, ACT.Identity,
                                                     scale=is_lo[64 * axis:64 * axis + 64, 0:1])\
                                  .then_inc(s_rhi, 1)
                    for t in range(NT):
                        u = due(unit, s, AT[f"qk{t}"])
                        if u:
                            act.wait_ge(s_qk_ps, u.n * NT + t + 1)
                            b4 = unit(AT["qk0"] // HEADS + 2)
                            if t == 0 and active(b4):
                                wait_dma(act, s_qd, b4)
                                wait_dma(act, s_kd, b4)
                            nc.scalar.activation(qk_hl[u.r % 2][:, 0, t, :], ps_m[BANK[f"qk{t}"]][:, 0:TOK],
                                                 ACT.Identity, bias=bqk[:, layer_of(u, layer), t:t + 1])\
                              .then_inc(s_qkhi, 1)

            run(act, iteration)

        @block.vector
        def _(dve):
            nc.vector.memset(rel_raw[:, :, :, :], 0.0).then_inc(s_pad, 1)
            nc.vector.memset(halfpow[:, :], -0.5)
            nc.vector.memset(eps[:, :], EPS)
            for i in range(UNROLL):
                nc.vector.memset(v_st[i][:, :, :, :], VS)
            dve.wait_ge(s_const, 16 * 7)
            for i in range(UNROLL):
                for head in range(HEADS):
                    nc.vector.tensor_copy(k_st[i][R_REL:STACK, head, :], oh_raw[R_REL:STACK, :])
            for p, f in ((0, QS), (HQ * HD, KS * HD ** -0.5)):
                nc.vector.tensor_scalar(bqk[p:p + HQ * HD, :, :], bqk_raw[p:p + HQ * HD, :, :], f, None, ALU.mult)
            nc.vector.tensor_scalar(brow[:, :, 0, :], brow[:, :, 0, :], VS, None, ALU.mult)
            nc.vector.tensor_scalar(rel_raw[:, :, :, :], rel_raw[:, :, :, :], RS, None, ALU.mult)\
              .then_inc(s_wsc, 1)
            dve.wait_ge(s_wsc, 1)
            nc.vector.tensor_copy(rel_st[:, :, :, :], rel_raw[:, :, :, :]).then_inc(s_whi, 1)
            dve.wait_ge(s_whi, 1)
            nc.vector.tensor_tensor(rel_st[32:64, :, :, :], rel_raw[32:64, :, :, :], rel_st[32:64, :, :, :],
                                    ALU.subtract)
            for layer in range(LAYERS):
                dve.wait_ge(s_wraw[layer], 16)
                w_qk = w_raw[:, :, 0:2 * C].rearrange("p c (t x n) -> p c t x n", x=2, n=HQ * HD)
                for part, f in ((w_qk[:, :, :, 0], QS), (w_qk[:, :, :, 1], KS * HD ** -0.5),
                                (w_raw[:, :, 2 * C:4 * C], VS)):
                    nc.vector.tensor_scalar(part, part, f, None, ALU.mult).then_inc(s_wsc, 1)
                dve.wait_ge(s_wsc, 1 + 3 * (layer + 1))
                nc.vector.tensor_copy(w_hi[:, layer, :, :], w_raw[:, :, :]).then_inc(s_whi, 1)
                dve.wait_ge(s_whi, 2 + layer)
                nc.vector.tensor_tensor(w_lo[:, layer, :, :], w_raw[:, :, :], w_hi[:, layer, :, :],
                                        ALU.subtract).then_inc(s_wlo, 1)
            dve.wait_ge(s_wlo, LAYERS)
            nc.vector.memset(yo[0][:, :, :], 0.0).then_inc(s_setup, 1)

            def iteration(unit, layer):
                for s in range(HEADS):
                    u = due(unit, s, MAX_AT + s)
                    if u:
                        n = u.n * HEADS + s
                        dve.wait_ge(s_sm_ps, n + 1)
                        if s == 0:
                            wait(dve, s_mT_ps, u.n * 2 - 2)
                        nc.vector.reduce_max(mx[u.r % 2][:, s, :],
                                             ps_max[s % 2][0:HT, 0:2 * TOK].rearrange("p (q k) -> p q k", q=2),
                                             axis=AX.X).then_inc(s_mx, 1)
                    u = due(unit, s, BN_AT)
                    if u:
                        p2 = u.r % 2
                        dve.wait_ge(s_xT, u.n + 1)
                        for c in range(2):
                            nc.vector.bn_stats(bn6[p2][:, c, :], xT[p2][:, c, :]).then_inc(s_bn, 1)
                        dve.wait_ge(s_bn, u.n * 2 + 2)
                        wait(dve, s_g_ps, u.n - 1)
                        nc.vector.memset(anchor[:, 0:1], 0.0)
                        for c in range(2):
                            nc.vector.bn_aggr(mv[p2][:, c, :], bn6[p2][:, c, :]).then_inc(s_agg, 1)
                    u = due(unit, s, AT["ot"])
                    if u:
                        p2 = u.r % 2
                        ps = ps_m[BANK["ot"]][0:HT, 0:2 * HEADS * (HD + 1)].rearrange("p (n d) -> p n d", d=HD + 1)
                        dve.wait_ge(s_ot_ps, u.n + 1)
                        nc.vector.reciprocal(rsum[p2][:, :], ps[:, :, HD]).then_inc(s_rs, 1)
                        dve.wait_ge(s_rs, u.n + 1)
                        wait(dve, s_oT_ps, u.n - 1)
                        for h in range(2):
                            last = nc.vector.tensor_tensor(
                                on[p2][:, h, :].rearrange("p (c h d) -> p h c d", c=NT, d=HD),
                                ps[:, h * HEADS:h * HEADS + HEADS, 0:HD].rearrange("p (h c) d -> p h c d", c=NT),
                                rsum[p2][:, h * HEADS:h * HEADS + HEADS]
                                .rearrange("p (h c o) -> p h c o", c=NT, o=1).to_broadcast([HT, HQ, NT, HD]),
                                ALU.mult)
                        last.then_inc(s_on, 1)
                    u = due(unit, s, AT["oT"])
                    if u:
                        p2 = u.r % 2
                        dve.wait_ge(s_ohi, u.n + 1)
                        wait(dve, s_y_ps, u.n - 1)
                        nc.vector.tensor_tensor(oT_lo[p2][:, :, :],
                                                ps_m[BANK["oT"]][0:CC, 0:2 * TOK].rearrange("p (c t) -> p c t", c=2),
                                                oT_hi[p2][:, :, :], ALU.subtract).then_inc(s_olo, 1)
                    for n in range(len(RELB)):
                        u = due(unit, s, AT[f"rel{n}"] + REL_LO_LATER)
                        if u:
                            ps = ps_m[BANK[f"rel{n}"]]
                            rows, a0 = RELB[n], sum(RELB[:n])
                            b4 = unit((AT["rel0"] + REL_LO_LATER) // HEADS + 2)
                            if n == 0 and active(b4):
                                wait_dma(dve, s_rel, b4, 4)
                            hi = rel_views(rel_hi[u.r % 2], ps, rows, a0)
                            lo = rel_views(rel_hl[u.r % 2], ps, rows, a0)
                            dve.wait_ge(s_rhi, u.n * 6 + 2 * n + 2)
                            for (h, src), (l, _) in zip(hi, lo):
                                nc.vector.tensor_tensor(l, src, h, ALU.subtract).then_inc(s_rlo, 1)
                    for t in range(NT):
                        u = due(unit, s, AT[f"qk{t}"])
                        if u:
                            lay = layer_of(u, layer)
                            dve.wait_ge(s_qkhi, u.n * NT + t + 1)
                            b4 = unit(AT["qk0"] // HEADS + 2)
                            if t == 0 and active(b4):
                                wait_dma(dve, s_qd, b4)
                                wait_dma(dve, s_kd, b4)
                            nc.vector.scalar_tensor_tensor(
                                out=qk_hl[u.r % 2][:, 1, t, :], in0=ps_m[BANK[f"qk{t}"]][:, 0:TOK],
                                scalar=bqk[:, lay, t:t + 1], in1=qk_hl[u.r % 2][:, 0, t, :],
                                op0=ALU.add, op1=ALU.subtract).then_inc(s_qklo, 1)
                    for h in range(2):
                        u = due(unit, s, AT[f"v{h}"])
                        if u:
                            dve.wait_ge(s_v_ps, u.n * 2 + h + 1)
                            wait(dve, s_o_ps, (u.n - 3) * GROUPS)
                            nc.vector.tensor_tensor(
                                v_st[u.r][:, h, :, 0:HD],
                                ps_m[BANK[f"v{h}"]][0:HT, 0:C].rearrange("p (h d) -> p h d", d=HD),
                                brow[:, layer_of(u, layer), 0, :].rearrange("p (h d) -> p h d", d=HD), ALU.add)\
                              .then_inc(s_v, 1)
                    u = due(unit, s, AT["y"])
                    if u:
                        p2 = u.r % 2
                        dve.wait_ge(s_y_ps, u.n + 1)
                        dve.wait_ge(s_xb, u.n + 1)
                        b4 = unit(AT["y"] // HEADS + 2)
                        if active(b4):
                            wait_dma(dve, s_out, b4)
                        nc.vector.scalar_tensor_tensor(
                            out=yo[p2][:, :, :],
                            in0=ps_m[BANK["y"]][0:HT, 0:2 * C].rearrange("p (h c) -> p h c", h=2),
                            scalar=1.0 / VS, in1=xb[p2][:, :, :], op0=ALU.mult, op1=ALU.add).then_inc(s_y, 1)
                    u = due(unit, s, AT["g"])
                    if u:
                        p2 = u.r % 2
                        dve.wait_ge(s_g_ps, u.n + 1)
                        wait(dve, s_gp, u.n * 5 - 5)
                        nc.vector.tensor_copy(gsm[p2][:, :, :],
                                              ps_m[BANK["g"]][0:CC, 0:4].rearrange("p (c s) -> p c s", c=2))\
                          .then_inc(s_g, 1)

            run(dve, iteration)

        @block.gpsimd
        def _(pool):
            pool.wait_ge(s_setup, 1)

            def iteration(unit, layer):
                u = unit(LAG_A)
                if active(u):
                    p2 = u.r % 2
                    pool.wait_ge(s_g, u.n + 1)
                    nc.gpsimd.tensor_tensor(msq[p2][:, :], gsm[p2][:, :, 0], gsm[p2][:, :, 0], ALU.mult)\
                      .then_inc(s_gp, 1)
                    pool.wait_ge(s_gp, u.n * 5 + 1)
                    nc.gpsimd.tensor_tensor(gvar[p2][:, :], gsm[p2][:, :, 1], msq[p2][:, :], ALU.subtract)\
                      .then_inc(s_gp, 1)
                    pool.wait_ge(s_gp, u.n * 5 + 2)
                    nc.gpsimd.tensor_tensor(gvar[p2][:, :], gvar[p2][:, :], eps[:, :], ALU.add)\
                      .then_inc(s_gp, 1)
                    pool.wait_ge(s_gp, u.n * 5 + 3)
                    nc.gpsimd.tensor_tensor(rstd[p2][:, :], gvar[p2][:, :], halfpow[:, :], ALU.pow)\
                      .then_inc(s_gp, 1)
                    nc.gpsimd.tensor_scalar(nmean[p2][:, :], gsm[p2][:, :, 0], -1.0, None, ALU.mult)\
                      .then_inc(s_gp, 1)
                    pool.wait_ge(s_gp, u.n * 5 + 5)
                    nc.gpsimd.tensor_tensor(anchor[:, 1:3], eps[:, :], eps[:, :], ALU.add)
                    for c in range(2):
                        nc.gpsimd.tensor_scalar(xn[p2][:, c, :], xT[p2][:, c, :], nmean[p2][:, c:c + 1],
                                                rstd[p2][:, c:c + 1], ALU.add, ALU.mult).then_inc(s_xn, 1)
                    pool.wait_ge(s_xhi, u.n + 1)
                    nc.gpsimd.tensor_tensor(xn_lo[p2][:, :, :], xn[p2][:, :, :], xn_hi[p2][:, :, :],
                                            ALU.subtract).then_inc(s_xlo, 1)
                d = unit(LAG_D)
                if active(d):
                    lay = layer_of(d, layer)
                    wait_dma(pool, s_xd, d)
                    wait(pool, s_y, d.n - 1)
                    for h in range(2):
                        last = nc.gpsimd.tensor_tensor(xb[d.r % 2][:, h, :], xd[d.r % 2][:, h, :],
                                                       brow[:, lay, 1, :], ALU.add)
                    last.then_inc(s_xb, 1)
                n = unit(LAG_X)
                if active(n):
                    p2 = n.r % 2
                    pool.wait_ge(s_agg, n.n * 2 + 2)
                    nc.gpsimd.tensor_tensor(msq[p2][:, :], mv[p2][:, :, 0], mv[p2][:, :, 0], ALU.mult)\
                      .then_inc(s_sq, 1)
                    pool.wait_ge(s_sq, n.n + 1)
                    nc.gpsimd.tensor_tensor(mv[p2][:, :, 1], mv[p2][:, :, 1], msq[p2][:, :], ALU.add)\
                      .then_inc(s_mv, 1)

            run(pool, iteration)


def kernel(x, L0_conv_qkv_w, L0_conv_qkv_b, L0_conv_rel_pos_h, L0_conv_rel_pos_w, L0_conv_proj_w,
           L0_conv_proj_b, L1_conv_qkv_w, L1_conv_qkv_b, L1_conv_proj_w, L1_conv_proj_b,
           L1_conv_rel_pos_h, L1_conv_rel_pos_w):
    import numpy as np
    import concourse.bacc as bacc
    from concourse.bass_utils import run_bass_kernel_spmd

    def a(v):
        return np.asarray(v)

    def tile(t):
        q = t * HQ * HD + (np.arange(HQ)[None, :] * HD + np.arange(HD)[:, None]).reshape(-1)
        return np.concatenate([q, C + q])

    qk_cols = np.concatenate([tile(t) for t in range(NT)])

    def weights(qkv, proj):
        return np.concatenate([qkv[:, qk_cols], qkv[:, 2 * C:], proj], axis=1)

    w_all = np.stack([weights(a(L0_conv_qkv_w).T, a(L0_conv_proj_w).T),
                      weights(a(L1_conv_qkv_w), a(L1_conv_proj_w))])
    qkv_b = [a(L0_conv_qkv_b), a(L1_conv_qkv_b)]
    proj_b = [a(L0_conv_proj_b), a(L1_conv_proj_b)]
    b_qk = np.stack([b[qk_cols].reshape(NT, 128).T for b in qkv_b], axis=1)
    b_rows = np.stack([np.stack([b[2 * C:], p]) for b, p in zip(qkv_b, proj_b)])
    b_rows = np.broadcast_to(b_rows[None], (HT, LAYERS, 2, C))
    rel = np.stack([np.stack([a(h)[REL - 1::-1].T, a(w)[REL - 1::-1].T], axis=1) for h, w in
                    ((L0_conv_rel_pos_h, L0_conv_rel_pos_w), (L1_conv_rel_pos_h, L1_conv_rel_pos_w))], axis=1)
    rel = np.repeat(np.concatenate([rel] * 4, axis=0), 2, axis=-1)

    rows = np.arange(TOK) // SIDE == np.arange(SIDE)[:, None]
    cols = np.arange(TOK) % SIDE == np.arange(SIDE)[:, None]
    rows, cols = (np.repeat(part, 2, axis=0) * (KS / RS) for part in (rows, cols))
    onehot = np.concatenate([rows, np.zeros((RW - 2 * SIDE, TOK)), cols, np.full((1, TOK), KS)])
    onehot = onehot.astype(np.float32)
    lo_rows = (np.arange(128)[:, None] % 2).astype(np.float32)
    ident = np.eye(128, dtype=np.float32)
    group = np.arange(CC) // GROUP
    gmat = ((group[:, None] == group[None, :]) / GROUP).astype(np.float32)

    ins = {"x": a(x).reshape(SAMPLES, TOK, C), "w_all": w_all, "b_qk": b_qk, "b_rows": b_rows, "rel": rel,
           "onehot": onehot, "lo_rows": lo_rows, "ident": ident, "gmat": gmat}
    ins = {k: np.ascontiguousarray(v) for k, v in ins.items()}
    nc = bacc.Bacc("TRN2", target_bir_lowering=False, num_devices=1)
    args = [nc.dram_tensor(f"in_{k}", v.shape, mybir.dt.from_np(v.dtype), kind="ExternalInput").ap()
            for k, v in ins.items()]
    args.append(nc.dram_tensor("out_0", (SAMPLES, TOK, C), F32, kind="ExternalOutput").ap())
    attention_kernel(nc, *args)
    r = run_bass_kernel_spmd(nc, [{f"in_{k}": v for k, v in ins.items()}], core_ids=[0])
    return r.results[0]["out_0"].reshape(SAMPLES, SIDE, SIDE, C)
```

```python
from contextlib import ExitStack

import concourse.bass as bass
from concourse import mybir

F32 = mybir.dt.float32
F16 = mybir.dt.float16
ALU = mybir.AluOpType
ACT = mybir.ActivationFunctionType
AX = mybir.AxisListType

LAYERS = 2
SAMPLES = 64
UNITS = LAYERS * SAMPLES
SIDE = 14
TOK = SIDE * SIDE
HT = TOK // 2
HALF = SIDE // 2
C = 192
CC = C // 2
HEADS = 12
HD = C // HEADS
HQ = 64 // HD
NT = HEADS // HQ
HH = HEADS // 2
GROUP = C // 32
EPS = 1e-5
REL = 2 * SIDE - 1

QS = 32.0
KS = 32.0
RS = 4.0
VS = 32.0

RW = 32
R_REL = 4 * HD
R_MAX = R_REL + RW + 2 * SIDE
STACK = R_MAX + 1

PW = 32
HG = 4
GROUPS = HEADS // HG
RELB = (6, 6, 2)
RP = 2 * (SIDE - 1) + RW
UNROLL = 4


class Unit:

    def __init__(self, block, place):
        self.block = block + place // UNROLL
        self.r = place % UNROLL
        self.n = self.block * UNROLL + self.r
        self.fixed = isinstance(block, int)


def attention_kernel(nc, x, w_all, b_qk, b_rows, rel, onehot, lo_rows, ident_in, gmat_in, out):
    with ExitStack() as ctx:
        def sb(name, shape, dt=F32):
            return ctx.enter_context(nc.sbuf_tensor(name, shape, dt))

        def psum(name, shape):
            return ctx.enter_context(nc.psum_tensor(name, shape, F32))

        def sem(name):
            return ctx.enter_context(nc.semaphore(name))

        def sems(name, n=UNROLL):
            return [sem(f"{name}{i}") for i in range(n)]

        x1 = nc.dram_tensor("x1", [SAMPLES, TOK, C], F32).ap()
        q_dram = nc.dram_tensor("q_dram", [UNROLL, 2, HD, HQ, NT, TOK], F16).ap()
        k_dram = nc.dram_tensor("k_dram", [UNROLL, 2, HD, HQ, NT, TOK], F16).ap()

        ident = sb("ident", [128, 128])
        gmat = sb("gmat", [CC, CC])
        w_raw = sb("w_raw", [CC, 2, 4 * C])
        w_hi = sb("w_hi", [CC, LAYERS, 2, 4 * C], F16)
        w_lo = sb("w_lo", [CC, LAYERS, 2, 4 * C], F16)
        bqk_raw = sb("bqk_raw", [128, LAYERS, NT])
        bqk = sb("bqk", [128, LAYERS, NT])
        brow = sb("brow", [HT, LAYERS, 2, C])
        rel_raw = sb("rel_raw", [64, LAYERS, 2, RP])
        rel_st = sb("rel_st", [64, LAYERS, 2, RP], F16)
        oh_raw = sb("oh_raw", [128, TOK])
        is_lo = sb("is_lo", [128, 1])
        halfpow = sb("halfpow", [CC, 2])
        eps = sb("eps", [CC, 2])
        anchor = sb("anchor", [CC, 3])

        q_st = [sb(f"q_st{i}", [128, HEADS, 2, HT], F16) for i in range(4)]
        k_st = [sb(f"k_st{i}", [128, HEADS, TOK], F16) for i in range(4)]
        v_st = [sb(f"v_st{i}", [HT, 2, HEADS, PW]) for i in range(4)]

        def pair(name, shape, dt=F32):
            return [sb(f"{name}{i}", shape, dt) for i in range(2)]

        xa = pair("xa", [HT, 2, C])
        xT = pair("xT", [CC, 2, TOK])
        bn6 = pair("bn6", [CC, 2, 6])
        mv = pair("mv", [CC, 2, 2])
        gsm = pair("gsm", [CC, 2, 2])
        msq = pair("msq", [CC, 2])
        gvar = pair("gvar", [CC, 2])
        rstd = pair("rstd", [CC, 2])
        nmean = pair("nmean", [CC, 2])
        xn = pair("xn", [CC, 2, TOK])
        xn_hi = pair("xn_hi", [CC, 2, TOK], F16)
        xn_lo = pair("xn_lo", [CC, 2, TOK], F16)
        qk_hl = pair("qk_hl", [128, 2, NT, TOK], F16)
        rel_hi = pair("rel_hi", [128, HH, TOK], F16)
        rel_hl = pair("rel_hl", [128, HH, TOK], F16)
        mx = pair("mx", [HT, HEADS, 2])
        mrow = pair("mrow", [HEADS, 2, HT], F16)
        probs = [sb(f"probs{i}", [HT, 2, TOK]) for i in range(HEADS)]
        vr = pair("vr", [HT, 2, C])
        o_sb = pair("o_sb", [128, GROUPS, TOK])
        rsum = pair("rsum", [HT, 2 * HEADS])
        on = pair("on", [HT, 2, C])
        oT_hi = pair("oT_hi", [CC, 2, TOK], F16)
        oT_lo = pair("oT_lo", [CC, 2, TOK], F16)
        xd = pair("xd", [HT, 2, C])
        xb = pair("xb", [HT, 2, C])
        yr = pair("yr", [HT, 2, C])
        yo = pair("yo", [HT, 2, C])

        ps_max = [psum(f"ps_max{i}", [128, 512]) for i in range(2)]
        ps_sc = [psum(f"ps_sc{i}", [128, 512]) for i in range(2)]
        ps_o = psum("ps_o", [128, 512])
        ps_m = [psum(f"ps_m{i}", [128, 512]) for i in range(3)]

        s_const = sem("s_const")
        s_wraw = sems("s_wraw", 2)
        s_pad = sem("s_pad")
        s_wsc = sem("s_wsc")
        s_whi = sem("s_whi")
        s_wlo = sem("s_wlo")
        s_setup = sem("s_setup")
        s_x = sems("s_x")
        s_xT_ps = sem("s_xT_ps")
        s_xT = sem("s_xT")
        s_bn = sem("s_bn")
        s_agg = sem("s_agg")
        s_sq = sem("s_sq")
        s_mv = sem("s_mv")
        s_g_ps = sem("s_g_ps")
        s_g = sem("s_g")
        s_gp = sem("s_gp")
        s_xn = sem("s_xn")
        s_xhi = sem("s_xhi")
        s_xlo = sem("s_xlo")
        s_qk_ps = sem("s_qk_ps")
        s_v_ps = sem("s_v_ps")
        s_qkhi = sem("s_qkhi")
        s_qklo = sem("s_qklo")
        s_vr = sem("s_vr")
        s_v = sem("s_v")
        s_qd = sems("s_qd")
        s_kd = sems("s_kd")
        s_qst = sems("s_qst")
        s_kst = sems("s_kst")
        s_rel_ps = sem("s_rel_ps")
        s_rhi = sem("s_rhi")
        s_rlo = sem("s_rlo")
        s_rel = sems("s_rel")
        s_sm_ps = sem("s_sm_ps")
        s_mx = sem("s_mx")
        s_mT_ps = sem("s_mT_ps")
        s_mrow = sem("s_mrow")
        s_m = [sems(f"s_m{h}_") for h in range(2)]
        s_sc_ps = sem("s_sc_ps")
        s_p = sem("s_p")
        s_o_ps = sem("s_o_ps")
        s_o = sem("s_o")
        s_ot_ps = sem("s_ot_ps")
        s_rs = sem("s_rs")
        s_on = sem("s_on")
        s_oT_ps = sem("s_oT_ps")
        s_ohi = sem("s_ohi")
        s_olo = sem("s_olo")
        s_y_ps = sem("s_y_ps")
        s_xd = sems("s_xd")
        s_xb = sem("s_xb")
        s_yr = sem("s_yr")
        s_y = sem("s_y")
        s_out = sems("s_out")

        block = ctx.enter_context(nc.Block())

        def wait(eng, s, value):
            if not (isinstance(value, int) and value <= 0):
                eng.wait_ge(s, value)

        def wait_dma(eng, group, u, dmas=1):
            wait(eng, group[u.r], (u.block + 1) * (16 * dmas))

        def head_of(place):
            return place % NT * HQ + place // NT

        def active(u):
            return not u.fixed or 0 <= u.n < UNITS

        def layer_of(u, loop_layer):
            return loop_layer if not u.fixed else u.n // SAMPLES

        def run(eng, iteration):
            at = -1
            for layer in range(LAYERS):
                first = layer * SAMPLES
                start = first + UNROLL * (2 if layer == 0 else 1)
                stop = first + SAMPLES - UNROLL
                for i in range(at, start):
                    iteration(lambda lag, i=i: Unit(0, i - lag), layer)
                with eng.Fori(start // UNROLL, stop // UNROLL) as t:
                    eng.compute_val(t * UNROLL)
                    for r in range(UNROLL):
                        iteration(lambda lag, t=t, r=r: Unit(t, r - lag), layer)
                at = stop
            for i in range(at, UNITS + UNROLL):
                iteration(lambda lag, i=i: Unit(0, i - lag), LAYERS - 1)

        MAX_AT, EXP_AT = 2 * HEADS, 3 * HEADS
        PV_AT = {(0, 0): 42, (0, 1): 43, (1, 0): 48, (1, 1): 49, (2, 0): 51, (2, 1): 52}
        O_LATER = 1

        JOBS = [(12, "rel0", 1, (s_rlo, 3, 1)),
                (13, "rel1", 0, (s_rlo, 3, 2)),
                (37, "mT1", 2, (s_mrow, 2, 2)),
                (14, "rel2", 2, (s_rlo, 3, 3)),
                (16, "v1", 1, (s_vr, 2, 2)),
                (5, "qk0", 0, (s_qklo, NT, 1)),
                (5, "qk1", 2, (s_qklo, NT, 2)),
                (5, "qk2", 1, (s_qklo, NT, 3)),
                (-6, "xT", 2, (s_xT, 1, 1)),
                (54, "ot", 0, (s_on, 1, 1)),
                (30, "mT0", 1, (s_mrow, 2, 1)),
                (56, "oT", 1, (s_olo, 1, 1)),
                (9, "v0", 2, (s_vr, 2, 1)),
                (-2, "g", 2, (s_g, 1, 1)),
                (58, "y", 0, (s_yr, 1, 1))]
        ORDER = [name for _, name, _, _ in JOBS]
        AT = {name: at for at, name, _, _ in JOBS}
        BANK = {name: bank for _, name, bank, _ in JOBS}
        READ = {name: read for _, name, _, read in JOBS}
        ACT_LATER = {"mT": 0, "oT": 0, "xT": 0, "qk": 0, "v": 0, "y": 0,
                     "rel": (0, 0)}
        DVE_LATER = {"bn": 1, "g": 0, "ot": 0, "oT": 0, "qk": 0,
                     "rel": 1}
        XHI_AT = 2
        POOL_AT = {"group": -2, "xn": 0, "xlo": 3, "xb": 54, "mv": -5, "v0": 12, "v1": 19,
                   "y": 58}

        LAG_X, LAG_A, LAG_REL, LAG_MAX, LAG_C, LAG_D = -1, 0, 1, 2, 3, 4

        def due(unit, slot, at):
            u = unit(at // HEADS)
            return u if at % HEADS == slot and active(u) else None

        def bank_free(pe, unit, job):
            at = ORDER.index(job)
            for back in range(1, 6 * len(ORDER)):
                turns, k = divmod(at - back, len(ORDER))
                u = unit(AT[ORDER[k]] // HEADS - turns)
                if BANK[ORDER[k]] == BANK[job] and active(u):
                    s, per, which = READ[ORDER[k]]
                    wait(pe, s, u.n * per + which)
                    return

        def rel_views(dst, ps, n, a0):
            by_row = (dst[0:64, :, a0 * SIDE:(a0 + n) * SIDE].rearrange("p h (a b) -> p a h b", a=n),
                      ps[0:64, 0:n * HH * SIDE].rearrange("p (a h b) -> p a h b", a=n, h=HH))
            by_col = (dst[64:128, :, :].rearrange("p h (a b) -> p b h a", a=SIDE)[:, a0:a0 + n],
                      ps[64:128, 0:n * HH * SIDE].rearrange("p (b h a) -> p b h a", b=n, h=HH))
            return by_row, by_col

        @block.sync
        def _(sp):
            sp.dma_start(ident[:, :], ident_in).then_inc(s_const, 16)
            sp.dma_start(gmat[:, :], gmat_in).then_inc(s_const, 16)
            sp.dma_start(oh_raw[R_REL:STACK, :], onehot).then_inc(s_const, 16)
            sp.dma_start(is_lo[:, :], lo_rows).then_inc(s_const, 16)
            sp.dma_start(bqk_raw[:, :, :], b_qk).then_inc(s_const, 16)
            sp.dma_start(brow[:, :, :, :], b_rows).then_inc(s_const, 16)
            sp.wait_ge(s_pad, 1)
            sp.dma_start(rel_raw[:, :, :, 0:2 * REL], rel).then_inc(s_const, 16)
            for layer in range(LAYERS):
                if layer:
                    sp.wait_ge(s_wlo, layer)
                sp.dma_start(w_raw[:, :, :], w_all[layer].rearrange("(c p) n -> p c n", c=2))\
                  .then_inc(s_wraw[layer], 16)

            def tokens(dram):
                return dram.rearrange("o (h t) c -> t (o h) c", h=2)

            def iteration(unit, layer):
                n, u, e, m, c, d = (unit(lag) for lag in (LAG_X, LAG_A, LAG_REL, LAG_MAX, LAG_C, LAG_D))
                if active(n) and not n.fixed:
                    for value in (n.n, n.n - 1):
                        sp.compute_val(value)
                if active(n):
                    nl = layer_of(n, layer)
                    if nl:
                        wait_dma(sp, s_out, unit(LAG_X + SAMPLES))
                    src, at = (x, n.n) if not nl else (x1, n.n - SAMPLES)
                    wait(sp, s_xT_ps, n.n - 1)
                    sp.dma_start(xa[n.r % 2][:, :, :], tokens(src[bass.ds(at, 1)])).then_inc(s_x[n.r], 16)
                dl = layer_of(d, layer)
                if active(d):
                    src, at = (x, d.n) if not dl else (x1, d.n - SAMPLES)
                    wait(sp, s_xb, d.n - 1)
                    sp.dma_start(xd[d.r % 2][:, :, :], tokens(src[bass.ds(at, 1)])).then_inc(s_xd[d.r], 16)
                def maxima(unit_, half):
                    if active(unit_):
                        wait(sp, s_mrow, unit_.n * 2 + half + 1)
                        sp.dma_start(q_st[unit_.r][R_MAX:STACK, half * HH:half * HH + HH, :, :],
                                     mrow[unit_.r % 2][:, half, :]).then_inc(s_m[half][unit_.r], 16)

                def to_dram(unit_, dram, row, landed):
                    sp.dma_start(dram[unit_.r].rearrange("l d h c t -> (d h) l (c t)"),
                                 qk_hl[unit_.r % 2][row:row + HQ * HD, :, :, :]
                                 .rearrange("p l c t -> p l (c t)")).then_inc(landed[unit_.r], 16)

                maxima(c, 1)
                if active(e):
                    wait(sp, s_rlo, e.n * 3 + 3)
                    for axis in range(2):
                        rows = RW if axis == 0 else 2 * SIDE
                        for half in range(2):
                            p, r0 = 64 * axis + 32 * half, R_REL + RW * axis
                            sp.dma_start(q_st[e.r][r0:r0 + rows, half * HH:half * HH + HH, :, :],
                                         rel_hl[e.r % 2][p:p + rows, :, :]).then_inc(s_rel[e.r], 16)
                if active(u):
                    wait(sp, s_qklo, u.n * NT + NT)
                    to_dram(u, q_dram, 0, s_qd)
                maxima(m, 0)
                if active(u):
                    to_dram(u, k_dram, HQ * HD, s_kd)
                    wait_dma(sp, s_qd, u)
                    both = q_dram[u.r:u.r + 1].rearrange("o l d h c t -> o (l d) (h c t)")
                    sp.dma_start(q_st[u.r][0:R_REL, :, :, :],
                                 both.to_broadcast([2, 2 * HD, HEADS * TOK])).then_inc(s_qst[u.r], 16)
                if active(u):
                    wait_dma(sp, s_kd, u)
                    for part in range(2):
                        one = k_dram[u.r, part:part + 1].rearrange("l d h c t -> l d (h c t)")
                        sp.dma_start(k_st[u.r][2 * HD * part:2 * HD * part + 2 * HD, :, :],
                                     one.to_broadcast([2, HD, HEADS * TOK])).then_inc(s_kst[u.r], 16)
                if active(d):
                    wait(sp, s_y, d.n + 1)
                    dst, at = (x1, d.n) if not dl else (out, d.n - SAMPLES)
                    sp.dma_start(tokens(dst[bass.ds(at, 1)]), yo[d.r % 2][:, :, :]).then_inc(s_out[d.r], 16)

            run(sp, iteration)
            for r in range(UNROLL):
                sp.wait_ge(s_out[r], 16 * UNITS // UNROLL)

        @block.tensor
        def _(pe):
            pe.wait_ge(s_setup, 1)
            pe.wait_ge(s_const, 16 * 7)

            def split_product(dst, weights, moving, signal):
                terms = [(a, b, c) for c in range(2) for a, b in ((0, 0), (0, 1), (1, 0))]
                for n, (a, b, c) in enumerate(terms):
                    last = nc.tensor.matmul(dst, weights(a, c), moving(b, c),
                                            start=n == 0, stop=n == len(terms) - 1)
                if signal is not None:
                    last.then_inc(signal, 1)

            def job(name, unit, slot, layer):
                u = due(unit, slot, AT[name])
                if not u:
                    return
                lay = layer_of(u, layer)
                ps, p2 = ps_m[BANK[name]], u.r % 2
                w_part, x_part = (w_hi, w_lo), (xn_hi[p2], xn_lo[p2])
                if name == "xT":
                    wait_dma(pe, s_x, u)
                    bank_free(pe, unit, name)
                    for c in range(2):
                        for h in range(2):
                            last = nc.tensor.transpose(ps[0:CC, c * TOK + h * HT:c * TOK + h * HT + HT],
                                                       xa[p2][:, h, c * CC:c * CC + CC], ident[0:HT, 0:HT])
                    last.then_inc(s_xT_ps, 1)
                elif name == "g":
                    pe.wait_ge(s_mv, u.n + 1)
                    bank_free(pe, unit, name)
                    nc.tensor.matmul(ps[0:CC, 0:4], gmat[:, :], mv[p2][:, :, :], start=True, stop=True)\
                      .then_inc(s_g_ps, 1)
                elif name.startswith("qk"):
                    n0 = int(name[2]) * 128
                    pe.wait_ge(s_xlo, u.n + 1)
                    bank_free(pe, unit, name)
                    split_product(ps[:, 0:TOK], lambda a, c: w_part[a][:, lay, c, n0:n0 + 128],
                                  lambda b, c: x_part[b][:, c, :], s_qk_ps)
                elif name in ("v0", "v1"):
                    h = int(name[1])
                    pe.wait_ge(s_xlo, u.n + 1)
                    bank_free(pe, unit, name)
                    split_product(ps[0:HT, 0:C], lambda a, c: x_part[a][:, c, h * HT:h * HT + HT],
                                  lambda b, c: w_part[b][:, lay, c, 2 * C:3 * C], s_v_ps)
                elif name.startswith("rel"):
                    n = int(name[3])
                    rows = RELB[n]
                    if n == 0:
                        wait_dma(pe, s_qst, u)
                    bank_free(pe, unit, name)
                    nc.tensor.matmul(ps[0:CC, 511:512], w_hi[:, 0, 0, 0:CC], w_hi[:, 0, 0, 0:1],
                                     start=True, stop=True)
                    for i in range(rows):
                        at, a = i * HH * SIDE, sum(RELB[:n]) + i
                        for axis in range(2):
                            w = 2 * (SIDE - 1 - a)
                            for half in range(2):
                                q = q_st[u.r][0:R_REL, half * HH:half * HH + HH, :, :]\
                                    .rearrange("p h q t -> p h (q t)")
                                p = 64 * axis + 32 * half
                                last = nc.tensor.matmul(
                                    ps[p:p + RW, at:at + HH * SIDE], rel_st[:, lay, axis, w:w + RW],
                                    q[:, :, a * SIDE:a * SIDE + SIDE] if axis == 0 else q[:, :, a::SIDE],
                                    start=True, stop=True)
                    last.then_inc(s_rel_ps, 1)
                elif name.startswith("mT"):
                    half = int(name[2])
                    pe.wait_ge(s_mx, u.n * HEADS + HH * (half + 1))
                    bank_free(pe, unit, name)
                    nc.tensor.transpose(ps[0:HEADS, 0:HT],
                                        mx[p2][:, HH * half:HH * half + HH, :].rearrange("p h q -> p (h q)"),
                                        ident[0:HT, 0:HT])\
                      .then_inc(s_mT_ps, 1)
                elif name == "ot":
                    pe.wait_ge(s_o, u.n * GROUPS + GROUPS)
                    bank_free(pe, unit, name)
                    for h in range(2):
                        for g in range(GROUPS):
                            at = (h * GROUPS + g) * HG * (HD + 1)
                            last = nc.tensor.matmul(
                                ps[0:HT, at:at + HG * (HD + 1)], o_sb[p2][:, g, h * HT:h * HT + HT],
                                ident[:, :].rearrange("p (j x) -> p j x", x=PW)[:, :, 0:HD + 1],
                                start=True, stop=True)
                    last.then_inc(s_ot_ps, 1)
                elif name == "oT":
                    pe.wait_ge(s_on, u.n + 1)
                    bank_free(pe, unit, name)
                    for c in range(2):
                        for h in range(2):
                            last = nc.tensor.transpose(ps[0:CC, c * TOK + h * HT:c * TOK + h * HT + HT],
                                                       on[p2][:, h, c * CC:c * CC + CC], ident[0:HT, 0:HT])
                    last.then_inc(s_oT_ps, 1)
                elif name == "y":
                    pe.wait_ge(s_olo, u.n + 1)
                    bank_free(pe, unit, name)
                    o_part = (oT_hi[p2], oT_lo[p2])
                    for h in range(2):
                        split_product(ps[0:HT, h * C:h * C + C],
                                      lambda a, c: o_part[a][:, c, h * HT:h * HT + HT],
                                      lambda b, c: w_part[b][:, lay, c, 3 * C:4 * C],
                                      s_y_ps if h else None)

            def iteration(unit, layer):
                for s in range(HEADS):
                    u = due(unit, s, MAX_AT + s)
                    if u:
                        if s == 0:
                            wait_dma(pe, s_rel, u, 4)
                            wait_dma(pe, s_kst, u, 2)
                        wait(pe, s_mx, u.n * HEADS + s - 1)
                        for h in range(2):
                            last = nc.tensor.matmul(ps_max[s % 2][0:HT, h * TOK:h * TOK + TOK],
                                                    q_st[u.r][0:R_MAX, s, h, :],
                                                    k_st[u.r][0:R_MAX, s, :],
                                                    start=True, stop=True)
                        last.then_inc(s_sm_ps, 1)
                    u, head = due(unit, s, EXP_AT + s), s
                    if u:
                        if head % HH == 0:
                            wait_dma(pe, s_m[head // HH], u)
                        wait(pe, s_p, u.n * HEADS + head - 1)
                        for kt in range(2):
                            last = nc.tensor.matmul(ps_sc[head % 2][0:HT, kt * TOK:kt * TOK + TOK],
                                                    k_st[u.r][0:STACK, head, kt * HT:kt * HT + HT],
                                                    q_st[u.r][0:STACK, head, :, :],
                                                    start=True, stop=True)
                        last.then_inc(s_sc_ps, 1)
                    for name in ORDER:
                        job(name, unit, s, layer)
                    for (g, kt), at in PV_AT.items():
                        u = due(unit, s, at)
                        if u:
                            n = u.n * GROUPS + g
                            if kt == 0:
                                wait(pe, s_v, u.n * 2 + 2)
                                wait(pe, s_p, u.n * HEADS + HG * g + HG)
                                wait(pe, s_o, n)
                            for j in range(HG):
                                head = HG * g + j
                                p = probs[head]
                                last = nc.tensor.matmul(ps_o[32 * j:32 * j + 32, 0:TOK],
                                                        v_st[u.r][:, kt, head_of(head), :], p[:, kt, :],
                                                        start=kt == 0, stop=kt == 1)
                            if kt == 1:
                                last.then_inc(s_o_ps, 1)

            run(pe, iteration)

        @block.scalar
        def _(act):
            act.wait_ge(s_setup, 1)

            def iteration(unit, layer):
                for s in range(HEADS):
                    for g in range(GROUPS):
                        u = due(unit, s, PV_AT[g, 1] + O_LATER)
                        if u:
                            act.wait_ge(s_o_ps, u.n * GROUPS + g + 1)
                            wait(act, s_ot_ps, u.n - 1)
                            nc.scalar.copy(o_sb[u.r % 2][:, g, :], ps_o[:, 0:TOK]).then_inc(s_o, 1)
                    u, head = due(unit, s, EXP_AT + s), s
                    if u:
                        n = u.n * HEADS + head
                        wait(act, s_sc_ps, n + 1)
                        wait(act, s_o_ps, u.n * GROUPS + head // HG - 2)
                        nc.scalar.activation(
                            probs[head][:, :, :],
                            ps_sc[head % 2][0:HT, 0:2 * TOK].rearrange("p (k t) -> p k t", k=2),
                            ACT.Exp, scale=1.0 / (QS * KS)).then_inc(s_p, 1)
                    for t in range(NT):
                        u = due(unit, s, AT[f"qk{t}"] + ACT_LATER["qk"])
                        if u:
                            act.wait_ge(s_qk_ps, u.n * NT + t + 1)
                            b4 = unit((AT["qk0"] + ACT_LATER["qk"]) // HEADS + 2)
                            if t == 0 and active(b4):
                                wait_dma(act, s_qd, b4)
                                wait_dma(act, s_kd, b4)
                            nc.scalar.activation(qk_hl[u.r % 2][:, 0, t, :], ps_m[BANK[f"qk{t}"]][:, 0:TOK],
                                                 ACT.Identity, bias=bqk[:, layer_of(u, layer), t:t + 1])\
                              .then_inc(s_qkhi, 1)
                    u = due(unit, s, XHI_AT)
                    if u:
                        act.wait_ge(s_xn, u.n * 2 + 2)
                        wait(act, s_v_ps, u.n * 2 - 2)
                        nc.scalar.copy(xn_hi[u.r % 2][:, :, :], xn[u.r % 2][:, :, :]).then_inc(s_xhi, 1)
                    for half in range(2):
                        name = f"mT{half}"
                        u = due(unit, s, AT[name] + ACT_LATER["mT"])
                        if u:
                            act.wait_ge(s_mT_ps, u.n * 2 + half + 1)
                            before = unit((AT[name] + ACT_LATER["mT"]) // HEADS + 2)
                            if active(before):
                                wait_dma(act, s_m[half], before)
                            nc.scalar.activation(mrow[u.r % 2][:, half, :], ps_m[BANK[name]][0:HEADS, 0:HT],
                                                 ACT.Copy, scale=-1.0 / KS).then_inc(s_mrow, 1)
                    u = due(unit, s, AT["oT"] + ACT_LATER["oT"])
                    if u:
                        act.wait_ge(s_oT_ps, u.n + 1)
                        wait(act, s_y_ps, u.n - 1)
                        nc.scalar.copy(oT_hi[u.r % 2][:, :, :],
                                       ps_m[BANK["oT"]][0:CC, 0:2 * TOK].rearrange("p (c t) -> p c t", c=2))\
                          .then_inc(s_ohi, 1)
                    u = due(unit, s, AT["xT"] + ACT_LATER["xT"])
                    if u:
                        act.wait_ge(s_xT_ps, u.n + 1)
                        wait(act, s_xn, u.n * 2 - 2)
                        nc.scalar.copy(xT[u.r % 2][:, :, :],
                                       ps_m[BANK["xT"]][0:CC, 0:2 * TOK].rearrange("p (c t) -> p c t", c=2))\
                          .then_inc(s_xT, 1)
                    for n in range(len(RELB)):
                        u = due(unit, s, AT[f"rel{n}"] + ACT_LATER["rel"][0])
                        if u:
                            act.wait_ge(s_rel_ps, u.n * 3 + n + 1)
                            b4 = unit((AT["rel0"] + ACT_LATER["rel"][0]) // HEADS + 2)
                            if n == 0 and active(b4):
                                wait_dma(act, s_rel, b4, 4)
                            dst, src = rel_views(rel_hi[u.r % 2], ps_m[BANK[f"rel{n}"]], RELB[n], sum(RELB[:n]))[0]
                            nc.scalar.activation(dst, src, ACT.Identity, scale=is_lo[0:64, 0:1])
                    u = due(unit, s, AT["y"] + ACT_LATER["y"])
                    if u:
                        act.wait_ge(s_y_ps, u.n + 1)
                        wait(act, s_y, u.n - 1)
                        nc.scalar.activation(yr[u.r % 2][:, :, :],
                                             ps_m[BANK["y"]][0:HT, 0:2 * C].rearrange("p (h c) -> p h c", h=2),
                                             ACT.Copy, scale=1.0 / VS).then_inc(s_yr, 1)
                    for n in range(len(RELB)):
                        u = due(unit, s, AT[f"rel{n}"] + ACT_LATER["rel"][1])
                        if u:
                            act.wait_ge(s_rel_ps, u.n * 3 + n + 1)
                            b4 = unit((AT["rel0"] + ACT_LATER["rel"][1]) // HEADS + 2)
                            if n == 0 and active(b4):
                                wait_dma(act, s_rel, b4, 4)
                            dst, src = rel_views(rel_hi[u.r % 2], ps_m[BANK[f"rel{n}"]], RELB[n], sum(RELB[:n]))[1]
                            nc.scalar.activation(dst, src, ACT.Identity, scale=is_lo[64:128, 0:1])\
                              .then_inc(s_rhi, 1)
                    for h in range(2):
                        u = due(unit, s, AT[f"v{h}"] + ACT_LATER["v"])
                        if u:
                            act.wait_ge(s_v_ps, u.n * 2 + h + 1)
                            wait(act, s_v, u.n * 2 + h - 3)
                            nc.scalar.copy(vr[u.r % 2][:, h, :], ps_m[BANK[f"v{h}"]][0:HT, 0:C]).then_inc(s_vr, 1)

            run(act, iteration)

        @block.vector
        def _(dve):
            nc.vector.memset(rel_raw[:, :, :, :], 0.0).then_inc(s_pad, 1)
            nc.vector.memset(halfpow[:, :], -0.5)
            nc.vector.memset(eps[:, :], EPS)
            for i in range(UNROLL):
                nc.vector.memset(v_st[i][:, :, :, :], VS)
            dve.wait_ge(s_const, 16 * 7)
            for i in range(UNROLL):
                for head in range(HEADS):
                    nc.vector.tensor_copy(k_st[i][R_REL:STACK, head, :], oh_raw[R_REL:STACK, :])
            for p, f in ((0, QS), (HQ * HD, KS * HD ** -0.5)):
                nc.vector.tensor_scalar(bqk[p:p + HQ * HD, :, :], bqk_raw[p:p + HQ * HD, :, :], f, None, ALU.mult)
            nc.vector.tensor_scalar(brow[:, :, 0, :], brow[:, :, 0, :], VS, None, ALU.mult)
            nc.vector.tensor_scalar(rel_raw[:, :, :, :], rel_raw[:, :, :, :], RS, None, ALU.mult)\
              .then_inc(s_wsc, 1)
            dve.wait_ge(s_wsc, 1)
            nc.vector.tensor_copy(rel_st[:, :, :, :], rel_raw[:, :, :, :]).then_inc(s_whi, 1)
            dve.wait_ge(s_whi, 1)
            nc.vector.tensor_tensor(rel_st[32:64, :, :, :], rel_raw[32:64, :, :, :], rel_st[32:64, :, :, :],
                                    ALU.subtract)
            for layer in range(LAYERS):
                dve.wait_ge(s_wraw[layer], 16)
                w_qk = w_raw[:, :, 0:2 * C].rearrange("p c (t x n) -> p c t x n", x=2, n=HQ * HD)
                for part, f in ((w_qk[:, :, :, 0], QS), (w_qk[:, :, :, 1], KS * HD ** -0.5),
                                (w_raw[:, :, 2 * C:4 * C], VS)):
                    nc.vector.tensor_scalar(part, part, f, None, ALU.mult).then_inc(s_wsc, 1)
                dve.wait_ge(s_wsc, 1 + 3 * (layer + 1))
                nc.vector.tensor_copy(w_hi[:, layer, :, :], w_raw[:, :, :]).then_inc(s_whi, 1)
                dve.wait_ge(s_whi, 2 + layer)
                nc.vector.tensor_tensor(w_lo[:, layer, :, :], w_raw[:, :, :], w_hi[:, layer, :, :],
                                        ALU.subtract).then_inc(s_wlo, 1)
            dve.wait_ge(s_wlo, LAYERS)
            nc.vector.memset(yo[0][:, :, :], 0.0).then_inc(s_setup, 1)

            def iteration(unit, layer):
                for s in range(HEADS):
                    u = due(unit, s, MAX_AT + s)
                    if u:
                        n = u.n * HEADS + s
                        dve.wait_ge(s_sm_ps, n + 1)
                        if s == 0:
                            wait(dve, s_mT_ps, u.n * 2 - 2)
                        nc.vector.reduce_max(mx[u.r % 2][:, s, :],
                                             ps_max[s % 2][0:HT, 0:2 * TOK].rearrange("p (q k) -> p q k", q=2),
                                             axis=AX.X).then_inc(s_mx, 1)
                    for t in range(NT):
                        u = due(unit, s, AT[f"qk{t}"] + DVE_LATER["qk"])
                        if u:
                            lay = layer_of(u, layer)
                            dve.wait_ge(s_qkhi, u.n * NT + t + 1)
                            b4 = unit((AT["qk0"] + DVE_LATER["qk"]) // HEADS + 2)
                            if t == 0 and active(b4):
                                wait_dma(dve, s_qd, b4)
                                wait_dma(dve, s_kd, b4)
                            nc.vector.scalar_tensor_tensor(
                                out=qk_hl[u.r % 2][:, 1, t, :], in0=ps_m[BANK[f"qk{t}"]][:, 0:TOK],
                                scalar=bqk[:, lay, t:t + 1], in1=qk_hl[u.r % 2][:, 0, t, :],
                                op0=ALU.add, op1=ALU.subtract).then_inc(s_qklo, 1)
                    u = due(unit, s, AT["xT"] + DVE_LATER["bn"])
                    if u:
                        p2 = u.r % 2
                        dve.wait_ge(s_xT, u.n + 1)
                        for c in range(2):
                            nc.vector.bn_stats(bn6[p2][:, c, :], xT[p2][:, c, :]).then_inc(s_bn, 1)
                        dve.wait_ge(s_bn, u.n * 2 + 2)
                        wait(dve, s_g_ps, u.n - 1)
                        nc.vector.memset(anchor[:, 0:1], 0.0)
                        for c in range(2):
                            nc.vector.bn_aggr(mv[p2][:, c, :], bn6[p2][:, c, :]).then_inc(s_agg, 1)
                    u = due(unit, s, AT["ot"] + DVE_LATER["ot"])
                    if u:
                        p2 = u.r % 2
                        ps = ps_m[BANK["ot"]][0:HT, 0:2 * HEADS * (HD + 1)].rearrange("p (n d) -> p n d", d=HD + 1)
                        dve.wait_ge(s_ot_ps, u.n + 1)
                        nc.vector.reciprocal(rsum[p2][:, :], ps[:, :, HD]).then_inc(s_rs, 1)
                        dve.wait_ge(s_rs, u.n + 1)
                        wait(dve, s_oT_ps, u.n - 1)
                        for h in range(2):
                            last = nc.vector.tensor_tensor(
                                on[p2][:, h, :].rearrange("p (c h d) -> p h c d", c=NT, d=HD),
                                ps[:, h * HEADS:h * HEADS + HEADS, 0:HD].rearrange("p (h c) d -> p h c d", c=NT),
                                rsum[p2][:, h * HEADS:h * HEADS + HEADS]
                                .rearrange("p (h c o) -> p h c o", c=NT, o=1).to_broadcast([HT, HQ, NT, HD]),
                                ALU.mult)
                        last.then_inc(s_on, 1)
                    for n in range(len(RELB)):
                        u = due(unit, s, AT[f"rel{n}"] + DVE_LATER["rel"])
                        if u:
                            b4 = unit((AT["rel0"] + DVE_LATER["rel"]) // HEADS + 2)
                            if n == 0 and active(b4):
                                wait_dma(dve, s_rel, b4, 4)
                            hi, lo = (rel_views(part[u.r % 2], ps_m[BANK[f"rel{n}"]], RELB[n], sum(RELB[:n]))
                                      for part in (rel_hi, rel_hl))
                            dve.wait_ge(s_rhi, u.n * 3 + n + 1)
                            for (h, src), (l, _) in zip(hi, lo):
                                last = nc.vector.tensor_tensor(l, src, h, ALU.subtract)
                            last.then_inc(s_rlo, 1)
                    u = due(unit, s, AT["oT"] + DVE_LATER["oT"])
                    if u:
                        p2 = u.r % 2
                        dve.wait_ge(s_ohi, u.n + 1)
                        wait(dve, s_y_ps, u.n - 1)
                        nc.vector.tensor_tensor(oT_lo[p2][:, :, :],
                                                ps_m[BANK["oT"]][0:CC, 0:2 * TOK].rearrange("p (c t) -> p c t", c=2),
                                                oT_hi[p2][:, :, :], ALU.subtract).then_inc(s_olo, 1)
                    u = due(unit, s, AT["g"] + DVE_LATER["g"])
                    if u:
                        p2 = u.r % 2
                        dve.wait_ge(s_g_ps, u.n + 1)
                        wait(dve, s_gp, u.n * 5 - 5)
                        nc.vector.tensor_copy(gsm[p2][:, :, :],
                                              ps_m[BANK["g"]][0:CC, 0:4].rearrange("p (c s) -> p c s", c=2))\
                          .then_inc(s_g, 1)

            run(dve, iteration)

        @block.gpsimd
        def _(pool):
            pool.wait_ge(s_setup, 1)

            def iteration(unit, layer):
                for s in range(HEADS):
                    u = due(unit, s, POOL_AT["v1"])
                    if u:
                        p2 = u.r % 2
                        pool.wait_ge(s_vr, u.n * 2 + 2)
                        wait(pool, s_o_ps, (u.n - 3) * GROUPS)
                        nc.gpsimd.tensor_tensor(
                            v_st[u.r][:, 1, :, 0:HD], vr[p2][:, 1, :].rearrange("p (h d) -> p h d", d=HD),
                            brow[:, layer_of(u, layer), 0, :].rearrange("p (h d) -> p h d", d=HD), ALU.add)\
                          .then_inc(s_v, 1)
                    u = due(unit, s, POOL_AT["xlo"])
                    if u:
                        p2 = u.r % 2
                        pool.wait_ge(s_xhi, u.n + 1)
                        nc.gpsimd.tensor_tensor(xn_lo[p2][:, :, :], xn[p2][:, :, :], xn_hi[p2][:, :, :],
                                                ALU.subtract).then_inc(s_xlo, 1)
                    u = due(unit, s, POOL_AT["group"])
                    if u:
                        p2 = u.r % 2
                        pool.wait_ge(s_g, u.n + 1)
                        nc.gpsimd.tensor_tensor(msq[p2][:, :], gsm[p2][:, :, 0], gsm[p2][:, :, 0], ALU.mult)\
                          .then_inc(s_gp, 1)
                        pool.wait_ge(s_gp, u.n * 5 + 1)
                        nc.gpsimd.tensor_tensor(gvar[p2][:, :], gsm[p2][:, :, 1], msq[p2][:, :], ALU.subtract)\
                          .then_inc(s_gp, 1)
                        pool.wait_ge(s_gp, u.n * 5 + 2)
                        nc.gpsimd.tensor_tensor(gvar[p2][:, :], gvar[p2][:, :], eps[:, :], ALU.add)\
                          .then_inc(s_gp, 1)
                        pool.wait_ge(s_gp, u.n * 5 + 3)
                        nc.gpsimd.tensor_tensor(rstd[p2][:, :], gvar[p2][:, :], halfpow[:, :], ALU.pow)\
                          .then_inc(s_gp, 1)
                        nc.gpsimd.tensor_scalar(nmean[p2][:, :], gsm[p2][:, :, 0], -1.0, None, ALU.mult)\
                          .then_inc(s_gp, 1)
                    u = due(unit, s, POOL_AT["v0"])
                    if u:
                        p2 = u.r % 2
                        pool.wait_ge(s_vr, u.n * 2 + 1)
                        wait(pool, s_o_ps, (u.n - 3) * GROUPS)
                        nc.gpsimd.tensor_tensor(
                            v_st[u.r][:, 0, :, 0:HD], vr[p2][:, 0, :].rearrange("p (h d) -> p h d", d=HD),
                            brow[:, layer_of(u, layer), 0, :].rearrange("p (h d) -> p h d", d=HD), ALU.add)\
                          .then_inc(s_v, 1)
                    u = due(unit, s, POOL_AT["mv"])
                    if u:
                        p2 = u.r % 2
                        pool.wait_ge(s_agg, u.n * 2 + 2)
                        nc.gpsimd.tensor_tensor(msq[p2][:, :], mv[p2][:, :, 0], mv[p2][:, :, 0], ALU.mult)\
                          .then_inc(s_sq, 1)
                        pool.wait_ge(s_sq, u.n + 1)
                        nc.gpsimd.tensor_tensor(mv[p2][:, :, 1], mv[p2][:, :, 1], msq[p2][:, :], ALU.add)\
                          .then_inc(s_mv, 1)
                    u = due(unit, s, POOL_AT["xn"])
                    if u:
                        p2 = u.r % 2
                        pool.wait_ge(s_gp, u.n * 5 + 5)
                        nc.gpsimd.tensor_tensor(anchor[:, 1:3], eps[:, :], eps[:, :], ALU.add)
                        for c in range(2):
                            nc.gpsimd.tensor_scalar(xn[p2][:, c, :], xT[p2][:, c, :], nmean[p2][:, c:c + 1],
                                                    rstd[p2][:, c:c + 1], ALU.add, ALU.mult).then_inc(s_xn, 1)
                    u = due(unit, s, POOL_AT["y"])
                    if u:
                        p2 = u.r % 2
                        pool.wait_ge(s_yr, u.n + 1)
                        pool.wait_ge(s_xb, u.n + 1)
                        b4 = unit(POOL_AT["y"] // HEADS + 2)
                        if active(b4):
                            wait_dma(pool, s_out, b4)
                        nc.gpsimd.tensor_tensor(yo[p2][:, :, :], yr[p2][:, :, :], xb[p2][:, :, :], ALU.add)\
                          .then_inc(s_y, 1)
                    u = due(unit, s, POOL_AT["xb"])
                    if u:
                        p2 = u.r % 2
                        lay = layer_of(u, layer)
                        wait_dma(pool, s_xd, u)
                        wait(pool, s_y, u.n - 1)
                        for h in range(2):
                            last = nc.gpsimd.tensor_tensor(xb[u.r % 2][:, h, :], xd[u.r % 2][:, h, :],
                                                           brow[:, lay, 1, :], ALU.add)
                        last.then_inc(s_xb, 1)

            run(pool, iteration)


def kernel(x, L0_conv_qkv_w, L0_conv_qkv_b, L0_conv_rel_pos_h, L0_conv_rel_pos_w, L0_conv_proj_w,
           L0_conv_proj_b, L1_conv_qkv_w, L1_conv_qkv_b, L1_conv_proj_w, L1_conv_proj_b,
           L1_conv_rel_pos_h, L1_conv_rel_pos_w):
    import numpy as np
    import concourse.bacc as bacc
    from concourse.bass_utils import run_bass_kernel_spmd

    def a(v):
        return np.asarray(v)

    def tile(t):
        q = t * HQ * HD + (np.arange(HQ)[None, :] * HD + np.arange(HD)[:, None]).reshape(-1)
        return np.concatenate([q, C + q])

    qk_cols = np.concatenate([tile(t) for t in range(NT)])

    def weights(qkv, proj):
        return np.concatenate([qkv[:, qk_cols], qkv[:, 2 * C:], proj], axis=1)

    w_all = np.stack([weights(a(L0_conv_qkv_w).T, a(L0_conv_proj_w).T),
                      weights(a(L1_conv_qkv_w), a(L1_conv_proj_w))])
    qkv_b = [a(L0_conv_qkv_b), a(L1_conv_qkv_b)]
    proj_b = [a(L0_conv_proj_b), a(L1_conv_proj_b)]
    b_qk = np.stack([b[qk_cols].reshape(NT, 128).T for b in qkv_b], axis=1)
    b_rows = np.stack([np.stack([b[2 * C:], p]) for b, p in zip(qkv_b, proj_b)])
    b_rows = np.broadcast_to(b_rows[None], (HT, LAYERS, 2, C))
    rel = np.stack([np.stack([a(h)[REL - 1::-1].T, a(w)[REL - 1::-1].T], axis=1) for h, w in
                    ((L0_conv_rel_pos_h, L0_conv_rel_pos_w), (L1_conv_rel_pos_h, L1_conv_rel_pos_w))], axis=1)
    rel = np.repeat(np.concatenate([rel] * 4, axis=0), 2, axis=-1)

    rows = np.arange(TOK) // SIDE == np.arange(SIDE)[:, None]
    cols = np.arange(TOK) % SIDE == np.arange(SIDE)[:, None]
    rows, cols = (np.repeat(part, 2, axis=0) * (KS / RS) for part in (rows, cols))
    onehot = np.concatenate([rows, np.zeros((RW - 2 * SIDE, TOK)), cols, np.full((1, TOK), KS)])
    onehot = onehot.astype(np.float32)
    lo_rows = (np.arange(128)[:, None] % 2).astype(np.float32)
    ident = np.eye(128, dtype=np.float32)
    group = np.arange(CC) // GROUP
    gmat = ((group[:, None] == group[None, :]) / GROUP).astype(np.float32)

    ins = {"x": a(x).reshape(SAMPLES, TOK, C), "w_all": w_all, "b_qk": b_qk, "b_rows": b_rows, "rel": rel,
           "onehot": onehot, "lo_rows": lo_rows, "ident": ident, "gmat": gmat}
    ins = {k: np.ascontiguousarray(v) for k, v in ins.items()}
    nc = bacc.Bacc("TRN2", target_bir_lowering=False, num_devices=1)
    args = [nc.dram_tensor(f"in_{k}", v.shape, mybir.dt.from_np(v.dtype), kind="ExternalInput").ap()
            for k, v in ins.items()]
    args.append(nc.dram_tensor("out_0", (SAMPLES, TOK, C), F32, kind="ExternalOutput").ap())
    attention_kernel(nc, *args)
    r = run_bass_kernel_spmd(nc, [{f"in_{k}": v for k, v in ins.items()}], core_ids=[0])
    return r.results[0]["out_0"].reshape(SAMPLES, SIDE, SIDE, C)
```
